# Optimizing a Trainium2 kernel written in Bass

```python
import numpy as np
import jax
import jax.numpy as jnp

def _softmax(x, axis=-1):
    return jax.nn.softmax(x, axis=axis)

def _gelu(x):
    return jax.nn.gelu(x, approximate=True)

def _silu(x):
    return jax.nn.silu(x)

def _sigmoid(x):
    return jax.nn.sigmoid(x)

def _layernorm(x, axis=-1, eps=1e-05):
    m = jnp.mean(x, axis=axis, keepdims=True)
    v = jnp.var(x, axis=axis, keepdims=True)
    return (x - m) / jnp.sqrt(v + eps)

def _scatter_add(tgt, idx, src, axis=0):
    return tgt.at[idx].add(src)

def _segment_sum(src, seg, n):
    return jax.ops.segment_sum(src, seg, n)
kernel_name = 'mk_vit_tower_cls_d1_tok_img768_r4_82a4fe'

def setup_inputs(seed: int=0):
    np.random.seed(seed)
    _w = jnp.asarray

    def _rec_inputs():
        import jax
        import jax.numpy as jnp
        _rk = jax.random.key(seed)
        x = -0.000222058 + 0.999998 * jax.random.normal(jax.random.fold_in(_rk, 1), (128, 3, 64, 64), jnp.float32)
        cls_tok = 0.02 * jax.random.normal(jax.random.fold_in(_rk, 5), (1, 1, 192), jnp.float32)
        return (x, cls_tok)
    x, cls_tok = _rec_inputs()

    def _L0_tok_setup():
        import jax, jax.numpy as jnp
        import numpy as np
        IMG = 64
        PS = 16
        C = 3
        ED = 192
        NP_SIDE = IMG // PS
        NUM_PATCHES = NP_SIDE * NP_SIDE
        PATCH_DIM = C * PS * PS
        key = jax.random.key(seed)
        k1, k2, k3, k4 = jax.random.split(key, 4)
        B = 128
        x = jax.random.normal(k1, (B, C, IMG, IMG), dtype=jnp.float32)
        bound = 1.0 / np.sqrt(PATCH_DIM)
        W = jax.random.uniform(k2, (ED, PATCH_DIM), minval=-bound, maxval=bound, dtype=jnp.float32)
        b = jax.random.uniform(k3, (ED,), minval=-bound, maxval=bound, dtype=jnp.float32)
        pos = jax.random.normal(k4, (1, NUM_PATCHES, ED), dtype=jnp.float32)
        return {'x': x, 'W': W, 'b': b, 'pos': pos}
    _L0_tok_all = _L0_tok_setup()
    _L0_tok_in = {k: v for k, v in _L0_tok_all.items() if k in ('W', 'b', 'pos')}
    del _L0_tok_all

    def _L0_attn_setup():
        import jax, jax.numpy as jnp
        import numpy as np
        NUM_HEADS = 12

        def _reference_tuple_inner(x, w_qkv, w_proj, b_proj):
            b, n, c = x.shape
            h = NUM_HEADS
            d = c // h
            qkv = (x @ w_qkv.T).reshape(b, n, 3, h, d).transpose(2, 0, 3, 1, 4)
            q, k, v = (qkv[0], qkv[1], qkv[2])
            q = jax.nn.elu(q) + 1.0
            k = jax.nn.elu(k) + 1.0
            kv = jnp.einsum('bhsd,bhse->bhde', k, v)
            z = 1.0 / jnp.einsum('bhsd,bhd->bhs', q, k.sum(axis=-2))
            out = jnp.einsum('bhde,bhsd,bhs->bhse', kv, q, z)
            out = out.transpose(0, 2, 1, 3).reshape(b, n, c)
            out = out @ w_proj.T + b_proj
            return (out, kv)
        key = jax.random.key(seed)
        k0, k1, k2 = jax.random.split(key, 3)
        b, n, c = (4, 1024, 192)
        x = jax.random.normal(k0, (b, n, c), dtype=jnp.float32)
        w_qkv = jax.random.normal(k1, (3 * c, c), dtype=jnp.float32) * 0.02
        w_proj = jax.random.normal(k2, (c, c), dtype=jnp.float32) * 0.02
        b_proj = jnp.zeros((c,), dtype=jnp.float32)
        return {'x': x, 'w_qkv': w_qkv, 'w_proj': w_proj, 'b_proj': b_proj}
    _L0_attn_all = _L0_attn_setup()
    _L0_attn_in = {k: v for k, v in _L0_attn_all.items() if k in ('w_qkv', 'w_proj', 'b_proj')}
    del _L0_attn_all

    def _L0_ffn_setup():
        import jax, jax.numpy as jnp
        import numpy as np
        B, S, D = (2, 256, 192)
        NF, NR, R, DS, K = (128, 128, 128, 64, 4)

        @jax.checkpoint
        def feature_fn(x, neurons, weights):
            all_h = jnp.einsum('bsd,ndr->bsnr', x, neurons)
            return jnp.einsum('bsnr,bsn->bsr', all_h, weights)

        @jax.checkpoint
        def restore_fn(h, neurons, weights):
            all_out = jnp.einsum('bsr,nrd->bsnd', h, neurons)
            return jnp.einsum('bsnd,bsn->bsd', all_out, weights)

        def topk_sparsify(weights, k):
            topk_vals, topk_idx = jax.lax.top_k(weights, k)
            N = weights.shape[-1]
            one_hot_mask = jax.nn.one_hot(topk_idx, N, dtype=weights.dtype)
            sparse = (one_hot_mask * topk_vals[..., jnp.newaxis]).sum(axis=-2)
            sparse = sparse / (sparse.sum(axis=-1, keepdims=True) + 1e-08)
            return (sparse, topk_idx)
        key = jax.random.key(seed)
        ks = jax.random.split(key, 8)
        x = jax.random.normal(ks[0], (B, S, D), jnp.float32)
        f_know = jax.random.normal(ks[1], (NF, D, R), jnp.float32) * 0.02
        r_know = jax.random.normal(ks[2], (NR, R, D), jnp.float32) * 0.02
        W_fk = jax.random.normal(ks[3], (D, DS), jnp.float32) * 0.02
        b_fk = jnp.zeros((DS,), jnp.float32)
        W_rk = jax.random.normal(ks[4], (D, DS), jnp.float32) * 0.02
        b_rk = jnp.zeros((DS,), jnp.float32)
        emb_fk = jax.random.normal(ks[5], (NF, DS), jnp.float32) * 0.02
        emb_rk = jax.random.normal(ks[6], (NR, DS), jnp.float32) * 0.02
        return {'x': x, 'f_know': f_know, 'r_know': r_know, 'W_fk': W_fk, 'b_fk': b_fk, 'W_rk': W_rk, 'b_rk': b_rk, 'emb_fk': emb_fk, 'emb_rk': emb_rk}
    _L0_ffn_all = _L0_ffn_setup()
    _L0_ffn_in = {k: v for k, v in _L0_ffn_all.items() if k in ('f_know', 'r_know', 'W_fk', 'b_fk', 'W_rk', 'b_rk', 'emb_fk', 'emb_rk')}
    del _L0_ffn_all
    return {'x': x, 'cls_tok': cls_tok, 'L0_tok_W': _L0_tok_in['W'], 'L0_tok_b': _L0_tok_in['b'], 'L0_tok_pos': _L0_tok_in['pos'], 'L0_attn_w_qkv': _L0_attn_in['w_qkv'], 'L0_attn_w_proj': _L0_attn_in['w_proj'], 'L0_attn_b_proj': _L0_attn_in['b_proj'], 'L0_ffn_f_know': _L0_ffn_in['f_know'], 'L0_ffn_r_know': _L0_ffn_in['r_know'], 'L0_ffn_W_fk': _L0_ffn_in['W_fk'], 'L0_ffn_b_fk': _L0_ffn_in['b_fk'], 'L0_ffn_W_rk': _L0_ffn_in['W_rk'], 'L0_ffn_b_rk': _L0_ffn_in['b_rk'], 'L0_ffn_emb_fk': _L0_ffn_in['emb_fk'], 'L0_ffn_emb_rk': _L0_ffn_in['emb_rk']}

def reference(x, cls_tok, L0_tok_W, L0_tok_b, L0_tok_pos, L0_attn_w_qkv, L0_attn_w_proj, L0_attn_b_proj, L0_ffn_f_know, L0_ffn_r_know, L0_ffn_W_fk, L0_ffn_b_fk, L0_ffn_W_rk, L0_ffn_b_rk, L0_ffn_emb_fk, L0_ffn_emb_rk):
    import jax
    import jax.numpy as jnp

    def _L0_tok_ref(x, W, b, pos):
        import jax, jax.numpy as jnp
        import numpy as np
        IMG = 64
        PS = 16
        C = 3
        ED = 192
        NP_SIDE = IMG // PS
        NUM_PATCHES = NP_SIDE * NP_SIDE
        PATCH_DIM = C * PS * PS
        B = x.shape[0]
        patches = x.reshape(B, C, NP_SIDE, PS, NP_SIDE, PS)
        patches = patches.transpose(0, 2, 4, 1, 3, 5)
        patches = patches.reshape(B, NUM_PATCHES, PATCH_DIM)
        emb = jnp.einsum('bpd,ed->bpe', patches, W) + b
        return emb + pos

    def _L0_attn_ref(x, w_qkv, w_proj, b_proj):
        import jax, jax.numpy as jnp
        import numpy as np
        NUM_HEADS = 12

        def _reference_tuple_inner(x, w_qkv, w_proj, b_proj):
            b, n, c = x.shape
            h = NUM_HEADS
            d = c // h
            qkv = (x @ w_qkv.T).reshape(b, n, 3, h, d).transpose(2, 0, 3, 1, 4)
            q, k, v = (qkv[0], qkv[1], qkv[2])
            q = jax.nn.elu(q) + 1.0
            k = jax.nn.elu(k) + 1.0
            kv = jnp.einsum('bhsd,bhse->bhde', k, v)
            z = 1.0 / jnp.einsum('bhsd,bhd->bhs', q, k.sum(axis=-2))
            out = jnp.einsum('bhde,bhsd,bhs->bhse', kv, q, z)
            out = out.transpose(0, 2, 1, 3).reshape(b, n, c)
            out = out @ w_proj.T + b_proj
            return (out, kv)
        return _reference_tuple_inner(x, w_qkv, w_proj, b_proj)[0]

    def _L0_ffn_ref(x, f_know, r_know, W_fk, b_fk, W_rk, b_rk, emb_fk, emb_rk):
        import jax, jax.numpy as jnp
        import numpy as np
        B, S, D = (2, 256, 192)
        NF, NR, R, DS, K = (128, 128, 128, 64, 4)

        @jax.checkpoint
        def feature_fn(x, neurons, weights):
            all_h = jnp.einsum('bsd,ndr->bsnr', x, neurons)
            return jnp.einsum('bsnr,bsn->bsr', all_h, weights)

        @jax.checkpoint
        def restore_fn(h, neurons, weights):
            all_out = jnp.einsum('bsr,nrd->bsnd', h, neurons)
            return jnp.einsum('bsnd,bsn->bsd', all_out, weights)

        def topk_sparsify(weights, k):
            topk_vals, topk_idx = jax.lax.top_k(weights, k)
            N = weights.shape[-1]
            one_hot_mask = jax.nn.one_hot(topk_idx, N, dtype=weights.dtype)
            sparse = (one_hot_mask * topk_vals[..., jnp.newaxis]).sum(axis=-2)
            sparse = sparse / (sparse.sum(axis=-1, keepdims=True) + 1e-08)
            return (sparse, topk_idx)
        emb_fk_n = emb_fk / (jnp.linalg.norm(emb_fk, axis=-1, keepdims=True) + 1e-08)
        emb_rk_n = emb_rk / (jnp.linalg.norm(emb_rk, axis=-1, keepdims=True) + 1e-08)
        logits_fk = jnp.einsum('bsd,nd->bsn', x @ W_fk + b_fk, emb_fk_n)
        logits_rk = jnp.einsum('bsd,nd->bsn', x @ W_rk + b_rk, emb_rk_n)
        w_fk, _ = topk_sparsify(jax.nn.softmax(logits_fk, axis=-1), K)
        w_rk, _ = topk_sparsify(jax.nn.softmax(logits_rk, axis=-1), K)
        h = feature_fn(x, f_know, w_fk)
        out = restore_fn(h, r_know, w_rk)
        return out
    h = _L0_tok_ref(x, L0_tok_W, L0_tok_b, L0_tok_pos)
    h = jnp.concatenate([jnp.broadcast_to(cls_tok, (h.shape[0], 1, h.shape[2])), h], axis=1)
    h = h + _L0_attn_ref(_layernorm(h, axis=-1), L0_attn_w_qkv, L0_attn_w_proj, L0_attn_b_proj)
    h = h + _L0_ffn_ref(_layernorm(h, axis=-1), L0_ffn_f_know, L0_ffn_r_know, L0_ffn_W_fk, L0_ffn_b_fk, L0_ffn_W_rk, L0_ffn_b_rk, L0_ffn_emb_fk, L0_ffn_emb_rk)
    return h

_drawn_inputs = setup_inputs


def setup_inputs(seed=0):
    import zlib

    import numpy as np

    out = dict(_drawn_inputs(seed))
    spreads = {'L0_attn_b_proj': (0.0, 0.1), 'L0_ffn_b_fk': (0.0, 0.718), 'L0_ffn_b_rk': (0.0, 0.707)}
    factors = {'cls_tok': 8.0,
     'L0_tok_b': 3.077,
     'L0_attn_w_qkv': 2.98,
     'L0_attn_w_proj': 3.047,
     'L0_ffn_f_know': 3.983,
     'L0_ffn_r_know': 3.997,
     'L0_ffn_W_fk': 4.124,
     'L0_ffn_W_rk': 4.057,
     'L0_ffn_emb_fk': 4.063,
     'L0_ffn_emb_rk': 4.05}
    for name, (base, spread) in spreads.items():
        noise = np.random.default_rng([zlib.crc32(name.encode()), seed]).standard_normal(out[name].shape)
        drawn = base * np.exp(spread * noise) if base else spread * noise
        out[name] = jnp.asarray(drawn.astype(out[name].dtype))
    for name, factor in factors.items():
        out[name] = (out[name] * factor).astype(out[name].dtype)
    return out
```

```python
import concourse.bass as bass
from concourse import mybir
from contextlib import ExitStack

B, NPOS, D = 128, 17, 192
IMGS = 7
P = IMGS * NPOS
NT = -(-B // IMGS)
KC = 6
HC = D // 2
NH, DH = 12, 16
NN, R, DS, K = 128, 128, 64, 4
BS = 64
NBLK = -(-(NT * P * K // BS + NN) // 8) * 8
ITS = NBLK // 4
ROWS = NBLK * BS
MAXB = -(-NT * P // BS)
CI, CM, CO, CU, CE, CB, CT, CP, CN = 0, 128, 247, 375, 503, 505, 505 + NBLK, 505 + NBLK + MAXB, 506 + NBLK + MAXB
NC = CN + 128


def constants(np):
    c = np.zeros((128, NC), np.float32)
    p = np.arange(128)
    c[:, CI:CI + 128] = np.eye(128)
    c[:, CM:CM + P] = (p[:, None] // NPOS) == (np.arange(P)[None] // NPOS)
    c[:, CO:CO + 128] = p[None]
    c[:, CU:CU + 128] = p[:, None] < p[None]
    c[:, CE] = (p // DH) % 2 == 0
    c[:, CE + 1] = (p // DH) % 2 == 1
    c[:, CB:CB + NBLK] = np.arange(NBLK)[None]
    c[:, CT:CT + MAXB] = BS * np.arange(MAXB)[None]
    c[:, CP] = ROWS + p
    c[:, CN:CN + 128] = p[:, None] <= p[None]
    return c


def vit_block(nc, xt_d, wt_d, bias_d, wqkv_d, wproj_d, bproj_d, wmid_d, bmid_d, emb_d, f_d, r_d, const_d, out_d):
    f32, bf16, i32, u32 = mybir.dt.float32, mybir.dt.bfloat16, mybir.dt.int32, mybir.dt.uint32
    ALU, ACT, AX = mybir.AluOpType, mybir.ActivationFunctionType, mybir.AxisListType
    ds = bass.ds
    ctx = ExitStack()
    with ctx:
        def sb(name, shape, dt=f32):
            return ctx.enter_context(nc.sbuf_tensor(name, shape, dt))

        def ps(name):
            return ctx.enter_context(nc.psum_tensor(name, [128, 512], f32))

        def sem(name):
            return ctx.enter_context(nc.semaphore(name))

        xs_d = nc.dram_tensor("xs", [ROWS, D], f32, kind="Internal").ap()
        ys_d = nc.dram_tensor("ys", [ROWS, R], f32, kind="Internal").ap()
        hs_d = nc.dram_tensor("hs", [ROWS, R], f32, kind="Internal").ap()
        zs_d = nc.dram_tensor("zs", [ROWS, D], f32, kind="Internal").ap()

        W = sb("W", [128, NN * 2 * R])
        CST = sb("CST", [128, NC])
        H = sb("H", [P, NT, D])
        X2 = sb("X2", [P, NT, D])
        M = sb("M", [P, NT, 2 * NN], bf16)
        MWORK = sb("MWORK", [128, (NT + 1) * NN])
        MPRE = MWORK[0:P, :].bitcast(bf16).rearrange("p (t n) -> p t n", n=2 * NN)
        XB = MWORK[:, 0:4 * D].rearrange("p (j a d) -> p j a d", j=2, a=2)
        YB = MWORK[0:BS, 4 * D:12 * D].rearrange("p (j b d) -> p j b d", j=2, b=4)
        TOPA = sb("TOPA", [P, NT, 2, K])
        IDXF = sb("IDXF", [P, NT, 2 * K])
        ZS = sb("ZS", [P, NT, 2])
        WTS = sb("WTS", [P, NT, 2, K])
        WSUM = sb("WSUM", [P, NT, 2])
        SLOTS = sb("SLOTS", [P, NT, 2 * K], i32)
        BASE = sb("BASE", [P, 2 * NN])
        RB = sb("RB", [P, 2 * NN])
        SLF = sb("SLF", [P, 2 * K])
        IDST = sb("IDST", [128, 2, K], i32)
        IDS2 = sb("IDS2", [128, 2, K], i32)
        XSTG = sb("XSTG", [128, 2, D])
        G = sb("G", [128, 2, K, D])
        ZERO = G[:].rearrange("p j k d -> p (j k d)")
        XBT = sb("XBT", [128, 2, 512])
        JUNK = XBT[0:P].rearrange("p j (k n) -> p (j k) n", n=NN)
        NB = sb("NB", [128, 2], bf16)
        NBF = sb("NBF", [128, 2])
        NBR = sb("NBR", [128, 2, 128], bf16)
        END = sb("END", [128, 2])
        GE = sb("GE", [128, 2, NBLK], bf16)
        ETF = sb("ETF", [1, 2, NBLK])
        ETAB = sb("ETAB", [1, 2, NBLK], i32)
        UB = sb("UB", [128, 128], bf16)
        UIB = sb("UIB", [128, 128], bf16)
        ONES = sb("ONES", [128, 128], bf16)
        THR = sb("THR", [128, MAXB])
        TICK = sb("TICK", [128, 5])

        used = [NN * R]

        def front(parts, shape, dt=f32):
            n = 1
            for s in shape:
                n *= s
            words = (n + 1) // 2 if dt == bf16 else n
            a = W[0:parts, used[0]:used[0] + words]
            used[0] += words + words % 2
            assert used[0] <= NN * 2 * R
            if dt != f32:
                a = a.bitcast(dt)
            names = "abcde"[:len(shape)]
            if len(shape) > 1:
                a = a.rearrange(f"p ({' '.join(names)}) -> p {' '.join(names)}", **dict(zip(names[1:], shape[1:])))
            return a

        XT = front(128, [2, KC, P])
        WT = front(128, [KC, D])
        WQKV = front(HC, [2, 3 * D])
        WPROJ = front(HC, [2, D])
        WMID = front(HC, [2, 2 * DS])
        BMID = front(128, [2])
        EMB = front(128, [2 * DS])
        ESQ = front(128, [2 * DS])
        ENS = front(128, [6, 2])
        EBD = front(128, [2 * NN])
        BIASE = front(P, [2, D])
        BPROJ = front(P, [D])
        LNC = front(P, [4])
        Y = front(P, [2, D])
        X2P = front(P, [2, D])
        YT = front(HC, [2, 2, P])
        Q = front(HC, [2, 2, 2, P])
        KT = front(HC, [2, 2, P])
        EX = front(HC, [4, P])
        RX = front(HC, [6, P])
        V17 = front(P, [2, NH, DH + 1])
        SM = front(P, [3, 2, 2, P])
        O = front(P, [2, D])
        RD = front(P, [NH])
        OT = front(HC, [2, 2, P])
        X2T = front(HC, [2, 2, P])
        MID = front(128, [2, P])
        L = front(P, [2, 2 * NN])
        EJ = front(P, [2, NN])
        ST = front(P, [2, 6])
        MV = front(P, [4, 2])
        RS = front(P, [4, 6])
        TOPP = front(P, [2, 2, 8])
        IDXP = front(P, [2, 2, 8], u32)
        IDXS = front(P, [2, 2 * K])
        NM = front(P, [2, 2])
        O8 = front(P, [2 * K, NN], bf16)
        A4 = front(P, [2, 2, NN], bf16)

        ID = CST[:, CI:CI + 128]
        IMASK = CST[0:P, CM:CM + P]
        IOTA = CST[0:P, CO:CO + NN]

        PB = [ps(f"PB{i}") for i in range(8)]
        PE_PROJ, PE_MID, PE_E = PB[0][0:P, 0:D], PB[1][:, 0:P], PB[4][0:P, 0:D]
        PE_YT = PB[3][0:HC, 0:2 * P].rearrange("p (c t) -> p c t", c=2)
        PE_X2T = PB[3][0:HC, 2 * P:4 * P].rearrange("p (c t) -> p c t", c=2)
        PE_QK = PB[2][0:HC, 0:4 * P].rearrange("p (c t) -> p c t", c=4)
        PE_S = [PB[3 + r][0:P, 0:4 * P].rearrange("p (c e t) -> p c e t", c=2, e=2) for r in range(3)]
        PE_V = PB[6][0:P, 0:D]
        PE_O = PB[6][0:P, 0:NH * (DH + 1)].rearrange("p (h d) -> p h d", h=NH)
        PE_OT = PB[5][0:HC, 0:2 * P].rearrange("p (c t) -> p c t", c=2)
        PE_L = PB[7][0:P, 0:2 * NN]

        names = """met0 met1 met2 met3 loaded consts_in zeros_set misc_set eb_sq eb_sum eb_sqrt eb_n1 eb_n2 eb_n3 eb_n4 eb_n5 eb_norm eb_T eb_ready
            x_in0 x_in1 emb_done emb_evac st1 stats1 rs1a rs1b rs1c rs1d rs1e rs1f rstd1 y_ready yT_done yT_evac qk_done act_qk qk_ready
            v_done v_ready s_done s_masked o_done o_rec o_normed oT_done oT_evac hb_ready proj_done h2_ready st2 stats2
            rs2a rs2b rs2c rs2d rs2e rs2f rstd2 x2_ready x2_kept x2T_done x2T_evac mid_done mid_evac log_done log_evac max_done idx_done
            topk_done idx_kept negmax z_done o8_done a4_done m_ready mpre_ready
            zeroed f_in f_in_upper r_in cnt_done nb_cmp nb_ready nbr_ready base_done base_ready end_ready ge_ready etab_done etf_ready etab_ready
            w1 w2 w3 w4 w5 w6 weights_ready
            rank_done rb_ready slf_ready slots_ready idst_ready xstg_ready
            scat0 scat1 gidx_ready gath0 gath1 comb1 comb2 comb3 hstg_ready ridx_ready rscat0 rscat1
            g2idx_ready g2a0 g2a1 comb21 comb22 comb23 comb24 out_ready out_stored""".split()
        S = {n: sem(n) for n in names}

        class Stage:
            def __init__(self, n):
                self.rows_in = [sem(f"{n}_rows_in{i}") for i in range(2)]
                self.rows_T, self.rows_T_evac = sem(f"{n}_rows_T"), sem(f"{n}_rows_T_evac")
                self.mm_done, self.mm_evac = sem(f"{n}_mm_done"), sem(f"{n}_mm_evac")
                self.stored = [sem(f"{n}_stored{i}") for i in range(2)]

        FEAT, REST = Stage("feat"), Stage("rest")
        block = ctx.enter_context(nc.Block())

        def need(eng, s, val):
            if not isinstance(val, int) or val > 0:
                eng.wait_ge(S[s] if isinstance(s, str) else s, val)

        def apart(eng):
            eng.wait_ge(S["consts_in"], 16)

        def tile_loop(eng, body, first, last, head, tail):
            assert (last + 1 - tail - first - head) % 2 == 0 and (first + head) % 2 == 0
            for i in range(first, first + head):
                body(i, i % 2)
            with eng.Fori(0, (last + 1 - tail - first - head) // 2) as u:
                body(u * 2 + (first + head), 0)
                body(u * 2 + (first + head + 1), 1)
            for i in range(last + 1 - tail, last + 1):
                body(i, i % 2)

        def front_loop(eng, body):
            tile_loop(eng, body, 0, NT + 2, 4, 4)

        def on(i, s):
            return not isinstance(i, int) or 0 <= i - s < NT

        def pair_sem(i, j):
            return 8 * (i - j) + 16

        @block.sync
        def _(sp):
            sp.dma_start(CST[:], const_d).then_inc(S["consts_in"], 16)
            for dst, src in ((WT, wt_d), (BIASE, bias_d), (WQKV, wqkv_d), (EMB, emb_d),
                             (BMID[:, 0:1], bmid_d), (WPROJ, wproj_d), (BPROJ, bproj_d), (WMID, wmid_d)):
                sp.dma_start(dst, src).then_inc(S["loaded"], 16)

            def load_x(i, j):
                need(sp, "emb_done", i - 1)
                sp.dma_start(XT[:, j], xt_d[ds(i, 1)].rearrange("a p c t -> (a p) c t")).then_inc(S[f"x_in{j}"], 16)

            tile_loop(sp, load_x, 0, NT - 1, 2, 1)

            sp.wait_ge(S["m_ready"], NT)
            sp.wait_ge(S["z_done"], NT)
            sp.wait_ge(S["topk_done"], NT)
            sp.wait_ge(S["negmax"], NT)
            for q in (2, 3):
                sp.dma_start(W[0:HC, q * 8192:(q + 1) * 8192], f_d[:, q * 8192:(q + 1) * 8192]).then_inc(S["f_in_upper"], 16)

            def experts(st, src, dst, n):
                def rows(i):
                    return src[ds(i * 4 * BS, 4 * BS)].rearrange("(a p) d -> p a d", p=128)

                def load(i, j):
                    sp.dma_start(XB[:, j, :, 0:n[0]], rows(i)).then_inc(st.rows_in[j], 16)

                load(0, 0)
                load(1, 1)

                def step(i, j):
                    if not isinstance(i, int) or i + 2 < ITS:
                        need(sp, st.rows_T, i + 1)
                        load(i + 2, j)
                    need(sp, st.mm_evac, i + 1)
                    sp.dma_start(dst[ds(i * 4 * BS, 4 * BS)].rearrange("(b p) d -> p b d", p=BS),
                                 YB[:, j, :, 0:n[1]]).then_inc(st.stored[j], 16)
                tile_loop(sp, step, 0, ITS - 1, 2, 2)

            sp.wait_ge(S["scat0"], 64 * ((NT + 1) // 2))
            sp.wait_ge(S["scat1"], 64 * (NT // 2))
            experts(FEAT, xs_d, ys_d, (D, R))
            sp.wait_ge(FEAT.mm_done, ITS)
            for q in range(4):
                sp.dma_start(W[:, q * 6144:(q + 1) * 6144], r_d[:, q * 6144:(q + 1) * 6144]).then_inc(S["r_in"], 16)
            sp.wait_ge(S["rscat0"], 64 * ((NT + 1) // 2))
            sp.wait_ge(S["rscat1"], 64 * (NT // 2))
            experts(REST, hs_d, zs_d, (R, D))

            def store(i, j):
                need(sp, "out_ready", i + 1)
                sp.dma_start(out_d[ds(i, 1)].rearrange("a t d -> (a t) d"),
                             H[:, ds(i, 1)].rearrange("p a d -> p (a d)")).then_inc(S["out_stored"], 16)
            tile_loop(sp, store, 0, NT - 1, 2, 1)
            sp.wait_ge(S["out_stored"], 16 * NT)

        @block.tensor
        def _(pe):
            mm, tr = nc.tensor.matmul, nc.tensor.transpose
            pe.wait_ge(S["consts_in"], 16)
            pe.wait_ge(S["loaded"], 8 * 16)
            pe.wait_ge(S["eb_norm"], 1)
            tr(PB[7][:, 0:128], ESQ, ID).then_inc(S["eb_T"], 1)

            def step(i, j):
                a, b, c, ja, jb, jc = i - 1, i - 2, i - 3, 1 - j, j, 1 - j
                if on(i, 2):
                    need(pe, "v_ready", b + 1)
                    need(pe, "o_normed", b)
                    for r in range(3):
                        need(pe, "s_masked", 3 * b + r + 1)
                        for cc in range(2):
                            for e in range(2):
                                h = 6 * cc + 2 * r + e
                                last = mm(PE_O[:, h], SM[:, r, cc, e], V17[:, jb, h], start=True, stop=True)
                    last.then_inc(S["o_done"], 1)
                if on(i, 3):
                    need(pe, "x2_ready", c + 1)
                    need(pe, "x2T_evac", c)
                    if on(i, 1):
                        need(pe, "yT_evac", a)
                    for cc in range(2):
                        last = tr(PE_X2T[:, cc], X2P[:, jc, cc * HC:(cc + 1) * HC], ID[0:P, 0:P])
                    last.then_inc(S["x2T_done"], 1)
                if on(i, 1):
                    need(pe, "y_ready", a + 1)
                    need(pe, "yT_evac", a)
                    need(pe, "s_masked", 3 * (a - 1) + 1)
                    for cc in range(2):
                        last = tr(PE_YT[:, cc], Y[:, ja, cc * HC:(cc + 1) * HC], ID[0:P, 0:P])
                    last.then_inc(S["yT_done"], 1)
                if on(i, 0):
                    need(pe, S[f"x_in{j}"], pair_sem(i, j))
                    need(pe, "emb_evac", i)
                    need(pe, "s_masked", 3 * (i - 2) + 2)
                    for k in range(KC):
                        last = mm(PE_E, XT[:, j, k], WT[:, k], start=(k == 0), stop=(k == KC - 1))
                    last.then_inc(S["emb_done"], 1)
                if on(i, 2):
                    need(pe, "o_normed", b + 1)
                    need(pe, "oT_evac", b)
                    for cc in range(2):
                        last = tr(PE_OT[:, cc], O[:, jb, cc * HC:(cc + 1) * HC], ID[0:P, 0:P])
                    last.then_inc(S["oT_done"], 1)
                if on(i, 3):
                    need(pe, "x2T_evac", c + 1)
                    need(pe, "mid_evac", c)
                    for cc in range(2):
                        last = mm(PE_MID, WMID[:, cc], X2T[:, jc, cc], start=(cc == 0), stop=(cc == 1))
                    last.then_inc(S["mid_done"], 1)
                if on(i, 1):
                    need(pe, "yT_evac", a + 1)
                    need(pe, "act_qk", a)
                    for m in range(4):
                        for cc in range(2):
                            last = mm(PE_QK[:, m], WQKV[:, cc, m * HC:(m + 1) * HC], YT[:, ja, cc], start=(cc == 0), stop=(cc == 1))
                    last.then_inc(S["qk_done"], 1)
                if on(i, 2):
                    need(pe, "oT_evac", b + 1)
                    need(pe, "h2_ready", b)
                    for cc in range(2):
                        last = mm(PE_PROJ, OT[:, jb, cc], WPROJ[:, cc], start=(cc == 0), stop=(cc == 1))
                    last.then_inc(S["proj_done"], 1)
                if on(i, 1):
                    need(pe, "v_ready", a)
                    for cc in range(2):
                        last = mm(PE_V, YT[:, ja, cc], WQKV[:, cc, 2 * D:3 * D], start=(cc == 0), stop=(cc == 1))
                    last.then_inc(S["v_done"], 1)
                if on(i, 3):
                    need(pe, "mid_evac", c + 1)
                    need(pe, "log_evac", c)
                    if isinstance(c, int) and c == 0:
                        pe.wait_ge(S["eb_ready"], 1)
                    mm(PE_L, MID[:, jc], EBD, start=True, stop=True).then_inc(S["log_done"], 1)
                if on(i, 1):
                    need(pe, "qk_ready", a + 1)
                    if on(i, 0):
                        need(pe, "emb_evac", i + 1)
                    for r in range(3):
                        need(pe, "s_masked", 3 * (a - 1) + r + 1)
                        for cc in range(2):
                            last = mm(PE_S[r][:, cc], KT[32 * r:32 * r + 32, ja, cc], Q[32 * r:32 * r + 32, ja, cc], start=True, stop=True)
                        last.then_inc(S["s_done"], 1)

            front_loop(pe, step)

            pe.wait_ge(S["mpre_ready"], NT)
            pe.wait_ge(S["misc_set"], 1)
            for q in range(2):
                last = mm(PB[0][:, q:q + 1], MPRE[:, NT, q * NN:(q + 1) * NN], ONES[0:P, 0:1], start=True, stop=True)
            last.then_inc(S["cnt_done"], 1)
            pe.wait_ge(S["nbr_ready"], 1)
            for q in range(2):
                mm(PB[1][0:P, q * NN:(q + 1) * NN], NBR[:, q, 0:P], UB[:], start=True, stop=True)
            mm(PB[0][:, 2:4], UIB[:], NB[:], start=True, stop=True).then_inc(S["base_done"], 1)
            pe.wait_ge(S["ge_ready"], 1)
            for q in range(2):
                last = mm(PB[6 + q][0:1, 0:NBLK], ONES[:, 0:1], GE[:, q], start=True, stop=True)
            last.then_inc(S["etab_done"], 1)

            def rank(i, j):
                need(pe, "rb_ready", i)
                mm(PB[2][0:P, 0:2 * NN], UB[0:P, 0:P], M[:, ds(i, 1)].rearrange("p a n -> p (a n)"), start=True, stop=False)
                mm(PB[2][0:P, 0:2 * NN], ONES[0:P, 0:P], MPRE[:, ds(i, 1)].rearrange("p a n -> p (a n)"),
                   start=False, stop=True).then_inc(S["rank_done"], 1)
            tile_loop(pe, rank, 0, NT - 1, 2, 1)

            def experts(st, q, na, m, n, wcol):
                def turn(i, j):
                    need(pe, st.rows_in[j], pair_sem(i, j))
                    need(pe, st.rows_T_evac, i - 1)
                    for a in range(2):
                        for cc in range(na):
                            t = a * na + cc
                            last = tr(PB[j][0:m, t * 128:(t + 1) * 128], XB[:, j, a, cc * m:(cc + 1) * m], ID)
                    last.then_inc(st.rows_T, 1)

                def product(i, j):
                    e = [pe.value_load(ETAB[0:1, q, ds(i * 4 + b, 1)], min_val=0, max_val=(NN - 1) * wcol) for b in range(4)]
                    need(pe, st.rows_T_evac, i + 1)
                    need(pe, st.mm_evac, i - 1)
                    for b in range(4):
                        o = PB[2 + 2 * j + b // 2][0:BS, (b % 2) * n:(b % 2) * n + n]
                        for cc in range(na):
                            col = ((b // 2) * na + cc) * 128 + (b % 2) * BS
                            last = mm(o, XBT[0:m, j, col:col + BS], W[0:m, ds(e[b] + cc * n, n)], start=(cc == 0), stop=(cc == na - 1))
                    last.then_inc(st.mm_done, 1)

                turn(0, 0)

                def step(i, j):
                    if not isinstance(i, int) or i + 1 < ITS:
                        turn(i + 1, 1 - j)
                    product(i, j)
                tile_loop(pe, step, 0, ITS - 1, 2, 2)

            pe.wait_ge(S["etab_ready"], 1)
            pe.wait_ge(S["f_in"], 32)
            pe.wait_ge(S["f_in_upper"], 32)
            experts(FEAT, 0, 2, HC, R, 2 * R)
            pe.wait_ge(S["r_in"], 64)
            experts(REST, 1, 1, 128, D, D)

        @block.scalar
        def _(act):
            A = nc.scalar.activation
            act.wait_ge(S["consts_in"], 16)
            act.wait_ge(S["loaded"], 8 * 16)
            act.wait_ge(S["eb_sum"], 1)
            A(ENS[:, 1], ENS[:, 0], ACT.Sqrt).then_inc(S["eb_sqrt"], 1)

            def step(i, j):
                a, b, c, ja, jb, jc = i - 1, i - 2, i - 3, 1 - j, j, 1 - j
                if on(i, 3):
                    need(act, "x2T_done", c + 1)
                    if on(i, 1):
                        need(act, "yT_done", a + 1)
                    need(act, "mid_done", c - 1)
                    nc.scalar.copy(X2T[:, jc], PE_X2T).then_inc(S["x2T_evac"], 1)
                if on(i, 1):
                    need(act, "yT_done", a + 1)
                    need(act, "v_done", a - 1)
                    nc.scalar.copy(YT[:, ja], PE_YT).then_inc(S["yT_evac"], 1)
                if on(i, 2):
                    need(act, "oT_done", b + 1)
                    need(act, "proj_done", b - 1)
                    nc.scalar.copy(OT[:, jb], PE_OT).then_inc(S["oT_evac"], 1)
                if on(i, 3):
                    need(act, "mid_done", c + 1)
                    need(act, "log_done", c - 1)
                    A(MID[:, jc], PE_MID, ACT.Identity, bias=BMID[:, 0:1]).then_inc(S["mid_evac"], 1)
                if on(i, 1):
                    need(act, "qk_done", a + 1)
                    need(act, "qk_ready", a)
                    A(EX, PE_QK, ACT.Exp)
                    A(RX[:, 0:2], PE_QK[:, 0:2], ACT.Relu, scale=CST[0:HC, CE:CE + 1])
                    A(RX[:, 2:4], PE_QK[:, 0:2], ACT.Relu, scale=CST[0:HC, CE + 1:CE + 2])
                    A(RX[:, 4:6], PE_QK[:, 2:4], ACT.Relu).then_inc(S["act_qk"], 1)
                    need(act, "v_done", a + 1)
                    need(act, "o_done", a - 1)
                    if isinstance(a, int) and a == 0:
                        act.wait_ge(S["misc_set"], 1)
                    nc.scalar.copy(V17[:, ja, :, 0:DH], PE_V.rearrange("p (h d) -> p h d", h=NH)).then_inc(S["v_ready"], 1)
                if on(i, 3):
                    need(act, "log_done", c + 1)
                    need(act, "idx_done", c - 1)
                    nc.scalar.copy(L[:, jc], PE_L).then_inc(S["log_evac"], 1)
                    need(act, "negmax", c + 1)
                    need(act, "z_done", c)
                    for q in range(2):
                        last = A(EJ[:, q], L[:, jc, q * NN:(q + 1) * NN], ACT.Exp, bias=NM[:, jc, q:q + 1],
                                 accum_out=ZS[:, ds(c, 1), q:q + 1].rearrange("p a q -> p (a q)"))
                    last.then_inc(S["z_done"], 1)

            front_loop(act, step)

            def stage_x(i, j):
                if not isinstance(i, int) or i >= 2:
                    act.wait_ge(S[f"scat{j}"], 32 * (i - j))
                else:
                    act.wait_ge(S["misc_set"], 1)
                nc.scalar.copy(XSTG[0:P, j], X2[:, ds(i, 1)].rearrange("p a d -> p (a d)")).then_inc(S["xstg_ready"], 1)
            tile_loop(act, stage_x, 0, NT - 1, 2, 1)
            act.wait_ge(S["w1"], 1)
            A(WTS[:], WTS[:], ACT.Exp).then_inc(S["w2"], 1)

            def experts(st, m, w):
                def step(i, j):
                    need(act, st.rows_T, i + 1)
                    need(act, st.mm_done, i - 1)
                    nc.scalar.copy(XBT[0:m, j, 0:w], PB[j][0:m, 0:w]).then_inc(st.rows_T_evac, 1)
                tile_loop(act, step, 0, ITS - 1, 2, 2)
            experts(FEAT, HC, 512)
            experts(REST, 128, 256)

        @block.vector
        def _(dve):
            V = nc.vector
            V.memset(ZERO[:], 0.0).then_inc(S["zeros_set"], 1)
            V.memset(ONES[:], 1.0)
            V.memset(LNC[:, 0:1], -0.5)
            V.memset(LNC[:, 1:2], 1e-5)
            V.memset(LNC[:, 2:3], 1.5)
            V.memset(XSTG[:], 0.0)
            V.memset(TICK[:], 0.0)
            V.memset(V17[:, :, :, DH:DH + 1], 1.0)
            V.memset(MPRE[:, 0], 0.0)
            dve.wait_ge(S["loaded"], 8 * 16)
            dve.wait_ge(S["consts_in"], 16)
            V.tensor_copy(UB[:], CST[:, CU:CU + 128])
            V.tensor_copy(UIB[:], CST[:, CN:CN + 128])
            for q in range(2):
                for k in range(K):
                    V.tensor_copy(IDST[:, q, k:k + 1], CST[:, CP:CP + 1])
                    V.tensor_copy(IDS2[:, q, k:k + 1], CST[:, CP:CP + 1])
            V.memset(EBD, 0.0)
            V.tensor_tensor(BIASE[:, 0], BIASE[:, 0], BIASE[:, 1], ALU.add).then_inc(S["misc_set"], 1)
            V.tensor_tensor(ESQ, EMB, EMB, ALU.mult).then_inc(S["eb_sq"], 1)
            dve.wait_ge(S["eb_sq"], 1)
            V.tensor_reduce(ENS[:, 0], ESQ.rearrange("p (q d) -> p q d", q=2), axis=AX.X, op=ALU.add).then_inc(S["eb_sum"], 1)
            dve.wait_ge(S["eb_sqrt"], 1)
            V.tensor_scalar(ENS[:, 2], ENS[:, 1], 1e-30, None, ALU.max).then_inc(S["eb_n1"], 1)
            dve.wait_ge(S["eb_n1"], 1)
            V.reciprocal(ENS[:, 3], ENS[:, 2]).then_inc(S["eb_n2"], 1)
            dve.wait_ge(S["eb_n2"], 1)
            V.tensor_tensor(ENS[:, 3], ENS[:, 3], ENS[:, 0], ALU.mult).then_inc(S["eb_n3"], 1)
            dve.wait_ge(S["eb_n3"], 1)
            V.tensor_tensor(ENS[:, 3], ENS[:, 3], ENS[:, 1], ALU.add).then_inc(S["eb_n4"], 1)
            dve.wait_ge(S["eb_n4"], 1)
            V.tensor_scalar(ENS[:, 4], ENS[:, 3], 0.5, 1e-8, ALU.mult, ALU.add).then_inc(S["eb_n5"], 1)
            dve.wait_ge(S["eb_n5"], 1)
            V.reciprocal(ENS[:, 5], ENS[:, 4]).then_inc(S["eb_n5"], 1)
            dve.wait_ge(S["eb_n5"], 2)
            V.tensor_tensor(ESQ.rearrange("p (q d) -> p q d", q=2), EMB.rearrange("p (q d) -> p q d", q=2),
                            ENS[:, 5].rearrange("p (q o) -> p q o", o=1).broadcast_to([128, 2, DS]), ALU.mult).then_inc(S["eb_norm"], 1)
            dve.wait_ge(S["eb_T"], 1)
            V.tensor_copy(EBD[0:DS, 0:NN], PB[7][0:DS, 0:NN])
            V.tensor_copy(EBD[DS:128, NN:2 * NN], PB[7][DS:128, 0:NN]).then_inc(S["eb_ready"], 1)
            dve.wait_ge(S["misc_set"], 1)

            def row(buf, t):
                return buf[:, ds(t, 1)].rearrange("p a d -> p (a d)")

            def step(i, j):
                a, b, c, ja, jb, jc = i - 1, i - 2, i - 3, 1 - j, j, 1 - j
                if on(i, 2):
                    need(dve, "o_done", b + 1)
                    V.reciprocal(RD, PE_O[:, :, DH]).then_inc(S["o_rec"], 1)
                    need(dve, "o_rec", b + 1)
                    need(dve, "oT_done", b - 1)
                    V.tensor_tensor(O[:, jb].rearrange("p (h d) -> p h d", h=NH), PE_O[:, :, 0:DH],
                                    RD.rearrange("p (h o) -> p h o", o=1).broadcast_to([P, NH, DH]), ALU.mult).then_inc(S["o_normed"], 1)
                if on(i, 0):
                    need(dve, "emb_done", i + 1)
                    V.tensor_tensor(row(H, i), PE_E, BIASE[:, 0], ALU.add).then_inc(S["emb_evac"], 1)
                    apart(dve)
                    need(dve, "emb_evac", i + 1)
                    apart(dve)
                    V.bn_stats(ST[:, 0], row(H, i)).then_inc(S["st1"], 1)
                    apart(dve)
                    need(dve, "st1", i + 1)
                    apart(dve)
                    V.bn_aggr(MV[:, j], ST[:, 0]).then_inc(S["stats1"], 1)
                if on(i, 1):
                    need(dve, "act_qk", a + 1)
                    for e in range(2):
                        V.scalar_tensor_tensor(Q[:, ja, :, e], EX[:, 0:2], CST[0:HC, CE + e:CE + e + 1], RX[:, 2 * e:2 * e + 2],
                                               ALU.min, ALU.add)
                    V.scalar_tensor_tensor(KT[:, ja], EX[:, 2:4], 1.0, RX[:, 4:6], ALU.min, ALU.add).then_inc(S["qk_ready"], 1)
                if on(i, 0):
                    need(dve, "rstd1", i + 1)
                    need(dve, "yT_done", i - 1)
                    V.tensor_scalar(Y[:, j], row(H, i), MV[:, j, 0:1], RS[:, j, 5:6], ALU.subtract, ALU.mult).then_inc(S["y_ready"], 1)
                if on(i, 2):
                    need(dve, "proj_done", b + 1)
                    need(dve, "hb_ready", b + 1)
                    V.tensor_tensor(row(H, b), PE_PROJ, row(H, b), ALU.add).then_inc(S["h2_ready"], 1)
                    apart(dve)
                    need(dve, "h2_ready", b + 1)
                    apart(dve)
                    V.bn_stats(ST[:, 1], row(H, b)).then_inc(S["st2"], 1)
                    apart(dve)
                    need(dve, "st2", b + 1)
                    apart(dve)
                    V.bn_aggr(MV[:, 2 + jb], ST[:, 1]).then_inc(S["stats2"], 1)
                if on(i, 3):
                    apart(dve)
                    need(dve, "log_evac", c + 1)
                    apart(dve)
                    for q in range(2):
                        last = V.max(TOPP[:, jc, q], L[:, jc, q * NN:(q + 1) * NN])
                    last.then_inc(S["max_done"], 1)
                    need(dve, "max_done", c + 1)
                    V.tensor_scalar(NM[:, jc], TOPP[:, jc, :, 0], -1.0, None, ALU.mult).then_inc(S["negmax"], 1)
                    for q in range(2):
                        last = V.max_index(IDXP[:, jc, q], TOPP[:, jc, q], L[:, jc, q * NN:(q + 1) * NN])
                    last.then_inc(S["idx_done"], 1)
                    V.tensor_copy(TOPA[:, ds(c, 1)].rearrange("p a q k -> p (a q) k"), TOPP[:, jc, :, 0:K])
                    need(dve, "idx_done", c + 1)
                    need(dve, "m_ready", c - 1)
                    need(dve, "idx_kept", c - 1)
                    V.tensor_copy(IDXS[:, jc].rearrange("p (q k) -> p q k", q=2), IDXP[:, jc, :, 0:K]).then_inc(S["topk_done"], 1)
                if on(i, 2):
                    need(dve, "rstd2", b + 1)
                    need(dve, "x2T_done", b - 1)
                    need(dve, "x2_kept", b - 1)
                    V.tensor_scalar(X2P[:, jb], row(H, b), MV[:, 2 + jb, 0:1], RS[:, 2 + jb, 5:6], ALU.subtract, ALU.mult).then_inc(S["x2_ready"], 1)
                if on(i, 1):
                    need(dve, "o_done", a)
                    for r in range(3):
                        need(dve, "s_done", 3 * a + r + 1)
                        V.tensor_tensor(SM[:, r].rearrange("p c e t -> p (c e) t"), PE_S[r].rearrange("p c e t -> p (c e) t"),
                                        IMASK.rearrange("p (o t) -> p o t", o=1).broadcast_to([P, 4, P]), ALU.mult).then_inc(S["s_masked"], 1)

            front_loop(dve, step)

            dve.wait_ge(S["cnt_done"], 1)
            for q in range(2):
                V.tensor_scalar(THR[:], CST[:, CT:CT + MAXB], PB[0][:, q:q + 1], 0.0, ALU.is_lt, ALU.add,
                                accum_out=NBF[:, q:q + 1]).then_inc(S["nb_cmp"], 1)
                dve.wait_ge(S["nb_cmp"], q + 1)
            V.tensor_copy(NB[:], NBF[:]).then_inc(S["nb_ready"], 1)
            for q in range(2):
                last = V.tensor_scalar(NBR[:, q], ONES[:], NBF[:, q:q + 1], None, ALU.mult)
            last.then_inc(S["nbr_ready"], 1)
            dve.wait_ge(S["base_done"], 1)
            V.tensor_scalar(BASE[:], PB[1][0:P, 0:2 * NN], float(BS), None, ALU.mult).then_inc(S["base_ready"], 1)
            V.tensor_copy(END[:], PB[0][:, 2:4]).then_inc(S["end_ready"], 1)
            dve.wait_ge(S["end_ready"], 1)
            for q in range(2):
                last = V.tensor_scalar(GE[:, q], CST[:, CB:CB + NBLK], END[:, q:q + 1], None, ALU.is_ge)
            last.then_inc(S["ge_ready"], 1)
            dve.wait_ge(S["etab_done"], 1)
            for q in range(2):
                last = V.tensor_scalar(ETF[:, q], PB[6 + q][0:1, 0:NBLK], float(NN - 1), float((2 * R, D)[q]), ALU.min, ALU.mult)
            last.then_inc(S["etf_ready"], 1)
            dve.wait_ge(S["etf_ready"], 1)
            V.tensor_copy(ETAB[:], ETF[:]).then_inc(S["etab_ready"], 1)

            def slots(i, j):
                need(dve, "rank_done", i + 1)
                V.tensor_tensor(RB[:], PB[2][0:P, 0:2 * NN], BASE[:], ALU.add).then_inc(S["rb_ready"], 1)
                need(dve, "rb_ready", i + 1)
                for k in range(2 * K):
                    q = k // K
                    last = V.scalar_tensor_tensor(JUNK[:, k], IOTA, IDXF[:, ds(i, 1), k:k + 1].rearrange("p a k -> p (a k)"),
                                                  RB[:, q * NN:(q + 1) * NN], ALU.is_equal, ALU.mult, accum_out=SLF[:, k:k + 1])
                last.then_inc(S["slf_ready"], 1)
                need(dve, "slf_ready", i + 1)
                V.tensor_copy(SLOTS[:, ds(i, 1)].rearrange("p a k -> p (a k)"), SLF[:]).then_inc(S["slots_ready"], 1)
                if not isinstance(i, int) or i >= 2:
                    dve.wait_ge(S[f"scat{j}"], 32 * (i - j))
                V.tensor_copy(IDST[0:P, j], SLF[:, 0:K]).then_inc(S["idst_ready"], 1)
            dve.wait_ge(S["base_ready"], 1)
            tile_loop(dve, slots, 0, NT - 1, 2, 1)

            dve.wait_ge(S["z_done"], NT)
            V.tensor_tensor(WTS[:], TOPA[:], TOPA[:, :, :, 0:1].broadcast_to([P, NT, 2, K]), ALU.subtract).then_inc(S["w1"], 1)
            V.reciprocal(ZS[:], ZS[:]).then_inc(S["w3"], 1)
            dve.wait_ge(S["w2"], 1)
            dve.wait_ge(S["w3"], 1)

            def over_k(t):
                return t[:].rearrange("p t (q o) -> p t q o", o=1).broadcast_to([P, NT, 2, K])
            V.tensor_tensor(WTS[:], WTS[:], over_k(ZS), ALU.mult).then_inc(S["w4"], 1)
            dve.wait_ge(S["w4"], 1)
            V.tensor_reduce(WSUM[:], WTS[:], axis=AX.X, op=ALU.add).then_inc(S["w5"], 1)
            dve.wait_ge(S["w5"], 1)
            V.tensor_scalar(WSUM[:], WSUM[:], 1e-8, None, ALU.add).then_inc(S["w5"], 1)
            dve.wait_ge(S["w5"], 2)
            V.reciprocal(WSUM[:], WSUM[:]).then_inc(S["w6"], 1)
            dve.wait_ge(S["w6"], 1)
            V.tensor_tensor(WTS[:], WTS[:], over_k(WSUM), ALU.mult).then_inc(S["weights_ready"], 1)

            def experts(st, n):
                def step(i, j):
                    need(dve, st.mm_done, i + 1)
                    if not isinstance(i, int) or i >= 2:
                        dve.wait_ge(st.stored[j], 8 * (i - j))
                    for u in range(2):
                        last = V.tensor_copy(YB[:, j, 2 * u:2 * u + 2, 0:n],
                                             PB[2 + 2 * j + u][0:BS, 0:2 * n].rearrange("p (b n) -> p b n", b=2))
                    last.then_inc(st.mm_evac, 1)
                tile_loop(dve, step, 0, ITS - 1, 2, 2)

            experts(FEAT, R)
            dve.wait_ge(S["weights_ready"], 1)

            def idx1(i, j):
                if not isinstance(i, int) or i >= 2:
                    dve.wait_ge(S[f"gath{j}"], 32 * (i - j))
                V.tensor_copy(IDST[0:P, j], SLOTS[:, ds(i, 1), 0:K].rearrange("p a k -> p (a k)")).then_inc(S["gidx_ready"], 1)

            def idx_h(i, j):
                if not isinstance(i, int) or i >= 2:
                    dve.wait_ge(S[f"rscat{j}"], 32 * (i - j))
                V.tensor_copy(IDS2[0:P, j], SLOTS[:, ds(i, 1), K:2 * K].rearrange("p a k -> p (a k)")).then_inc(S["ridx_ready"], 1)

            def weight(i, q, k):
                return WTS[:, ds(i, 1), q, k:k + 1].rearrange("p a k -> p (a k)")

            def combine1(i, j):
                dve.wait_ge(S[f"gath{j}"], 32 * (i - j) + 64)
                g, h = G[0:P, j], XSTG[0:P, j, 0:R]
                V.tensor_scalar(h, g[:, 0, 0:R], weight(i, 0, 0), None, ALU.mult).then_inc(S["comb1"], 1)
                need(dve, "comb1", i + 1)
                V.scalar_tensor_tensor(h, g[:, 1, 0:R], weight(i, 0, 1), h, ALU.mult, ALU.add).then_inc(S["comb2"], 1)
                need(dve, "comb2", i + 1)
                V.scalar_tensor_tensor(h, g[:, 2, 0:R], weight(i, 0, 2), h, ALU.mult, ALU.add).then_inc(S["comb3"], 1)
                need(dve, "comb3", i + 1)
                V.scalar_tensor_tensor(h, g[:, 3, 0:R], weight(i, 0, 3), h, ALU.mult, ALU.add).then_inc(S["hstg_ready"], 1)

            idx1(0, 0)
            idx1(1, 1)

            def middle(i, j):
                idx_h(i, j)
                combine1(i, j)
                if not isinstance(i, int) or i + 2 < NT:
                    idx1(i + 2, j)
            tile_loop(dve, middle, 0, NT - 1, 2, 3)

            experts(REST, D)

            def idx2(i, j):
                if not isinstance(i, int) or i >= 2:
                    dve.wait_ge(S[f"g2a{j}"], 32 * (i - j))
                V.tensor_copy(IDST[0:P, j], SLOTS[:, ds(i, 1), K:2 * K].rearrange("p a k -> p (a k)")).then_inc(S["g2idx_ready"], 1)

            def finish(i, j):
                dve.wait_ge(S[f"g2a{j}"], 32 * (i - j) + 64)
                for k in range(K):
                    last = V.scalar_tensor_tensor(row(H, i), G[0:P, j, k], weight(i, 1, k), row(H, i), ALU.mult, ALU.add)
                    if k < K - 1:
                        last.then_inc(S[f"comb2{k + 1}"], 1)
                        need(dve, f"comb2{k + 1}", i + 1)
                last.then_inc(S["out_ready"], 1)
                if not isinstance(i, int) or i + 2 < NT:
                    idx2(i + 2, j)
            idx2(0, 0)
            idx2(1, 1)
            tile_loop(dve, finish, 0, NT - 1, 2, 3)

        @block.gpsimd
        def _(pool):
            GP = nc.gpsimd
            pool.wait_ge(S["consts_in"], 16)
            pool.wait_ge(S["zeros_set"], 1)
            nz = ROWS // 128 // 8
            for dst, n in ((xs_d, D), (hs_d, R)):
                pool.dma_start(dst[0:ROWS].rearrange("(p s r) d -> p s (r d)", p=128, r=8),
                               ZERO[:, 0:8 * n].rearrange("p (o n) -> p o n", o=1).broadcast_to([128, nz, 8 * n])).then_inc(S["zeroed"], 16)
            for q in (0, 1):
                pool.dma_start(W[0:HC, q * 8192:(q + 1) * 8192], f_d[:, q * 8192:(q + 1) * 8192]).then_inc(S["f_in"], 16)
            pool.wait_ge(S["misc_set"], 1)

            def rstd(m, r, s, t):
                def c(k):
                    return RS[:, r, k:k + 1]
                GP.tensor_tensor(c(0), MV[:, m, 1:2], LNC[:, 1:2], ALU.add).then_inc(S[s + "a"], 1)
                need(pool, s + "a", t + 1)
                GP.tensor_tensor(c(1), c(0), LNC[:, 0:1], ALU.pow).then_inc(S[s + "b"], 1)
                need(pool, s + "b", t + 1)
                GP.tensor_tensor(c(2), c(1), c(1), ALU.mult).then_inc(S[s + "c"], 1)
                need(pool, s + "c", t + 1)
                GP.tensor_tensor(c(3), c(2), c(0), ALU.mult).then_inc(S[s + "d"], 1)
                need(pool, s + "d", t + 1)
                GP.tensor_tensor(c(4), c(3), LNC[:, 0:1], ALU.mult).then_inc(S[s + "e"], 1)
                need(pool, s + "e", t + 1)
                GP.tensor_tensor(c(3), c(4), LNC[:, 2:3], ALU.add).then_inc(S[s + "f"], 1)
                need(pool, s + "f", t + 1)
                GP.tensor_tensor(c(5), c(3), c(1), ALU.mult).then_inc(S["rstd" + s[2]], 1)

            def step(i, j):
                a, b, c, ja, jb, jc = i - 1, i - 2, i - 3, 1 - j, j, 1 - j
                if on(i, 0):
                    need(pool, "stats1", i + 1)
                    need(pool, "y_ready", i - 1)
                    rstd(j, j, "rs1", i)
                if on(i, 1):
                    need(pool, "y_ready", a + 1)
                    h = H[:, ds(a, 1)].rearrange("p a d -> p (a d)")
                    GP.tensor_tensor(h, h, BPROJ, ALU.add).then_inc(S["hb_ready"], 1)
                if on(i, 2):
                    need(pool, "stats2", b + 1)
                    need(pool, "x2_ready", b - 1)
                    rstd(2 + jb, 2 + jb, "rs2", b)
                    need(pool, "x2_ready", b + 1)
                    GP.tensor_copy(X2[:, ds(b, 1)].rearrange("p a d -> p (a d)"), X2P[:, jb]).then_inc(S["x2_kept"], 1)
                if on(i, 3):
                    need(pool, "topk_done", c + 1)
                    GP.tensor_copy(IDXF[:, ds(c, 1)].rearrange("p a k -> p (a k)"), IDXS[:, jc]).then_inc(S["idx_kept"], 1)
                    for k in range(2 * K):
                        last = GP.tensor_scalar(O8[:, k], IOTA, IDXS[:, jc, k:k + 1], None, ALU.is_equal)
                    last.then_inc(S["o8_done"], 1)
                    need(pool, "o8_done", c + 1)
                    o8 = O8.rearrange("p (q u v) n -> p q u v n", q=2, u=2)
                    for q in range(2):
                        last = GP.tensor_tensor(A4[:, q], o8[:, q, 0], o8[:, q, 1], ALU.add)
                    last.then_inc(S["a4_done"], 1)
                    need(pool, "a4_done", c + 1)
                    m = M[:, ds(c, 1)].rearrange("p a (q n) -> p (a q) n", q=2)
                    GP.tensor_tensor(m, A4[:, :, 0], A4[:, :, 1], ALU.add).then_inc(S["m_ready"], 1)
                    need(pool, "m_ready", c + 1)
                    need(pool, "mpre_ready", c)
                    GP.tensor_tensor(MPRE[:, ds(c + 1, 1)].rearrange("p a n -> p (a n)"), MPRE[:, ds(c, 1)].rearrange("p a n -> p (a n)"),
                                     M[:, ds(c, 1)].rearrange("p a n -> p (a n)"), ALU.add).then_inc(S["mpre_ready"], 1)

            front_loop(pool, step)

            def meet(site, i):
                need(pool, f"met{site}", i)
                GP.tensor_tensor(TICK[:, site:site + 1], TICK[:, 4:5], TICK[:, 4:5], ALU.add).then_inc(S[f"met{site}"], 1)

            def off(ids, j, k):
                return bass.IndirectOffsetOnAxis(ap=ids[:, j, k:k + 1], axis=0)

            pool.wait_ge(S["zeroed"], 32)

            def scatter_x(i, j):
                need(pool, "idst_ready", i + 1)
                need(pool, "xstg_ready", i + 1)
                meet(0, i)
                for k in range(K):
                    pool.indirect_dma_start(out=xs_d, out_offset=off(IDST, j, k), in_=XSTG[:, j], in_offset=None,
                                            bounds_check=ROWS - 1, oob_is_err=False).then_inc(S[f"scat{j}"], 16)
            tile_loop(pool, scatter_x, 0, NT - 1, 2, 1)

            pool.wait_ge(FEAT.stored[0], 16 * (ITS // 2))
            pool.wait_ge(FEAT.stored[1], 16 * (ITS // 2))

            def gather_y(i, j):
                need(pool, "gidx_ready", i + 1)
                need(pool, "hstg_ready", i - 1)
                meet(1, i)
                for k in range(K):
                    pool.indirect_dma_start(out=G[:, j, k, 0:R], out_offset=None, in_=ys_d, in_offset=off(IDST, j, k),
                                            bounds_check=ROWS - 1, oob_is_err=False).then_inc(S[f"gath{j}"], 16)

            gather_y(0, 0)

            def middle(i, j):
                if not isinstance(i, int) or i + 1 < NT:
                    gather_y(i + 1, 1 - j)
                need(pool, "ridx_ready", i + 1)
                need(pool, "hstg_ready", i + 1)
                meet(2, i)
                for k in range(K):
                    pool.indirect_dma_start(out=hs_d, out_offset=off(IDS2, j, k), in_=XSTG[:, j, 0:R], in_offset=None,
                                            bounds_check=ROWS - 1, oob_is_err=False).then_inc(S[f"rscat{j}"], 16)
            tile_loop(pool, middle, 0, NT - 1, 2, 3)

            pool.wait_ge(REST.stored[0], 16 * (ITS // 2))
            pool.wait_ge(REST.stored[1], 16 * (ITS // 2))

            def gather_z(i, j):
                need(pool, "g2idx_ready", i + 1)
                need(pool, "out_ready", i - 1)
                meet(3, i)
                for k in range(K):
                    pool.indirect_dma_start(out=G[:, j, k], out_offset=None, in_=zs_d, in_offset=off(IDST, j, k),
                                            bounds_check=ROWS - 1, oob_is_err=False).then_inc(S[f"g2a{j}"], 16)
            tile_loop(pool, gather_z, 0, NT - 1, 2, 1)


def kernel(x, cls_tok, L0_tok_W, L0_tok_b, L0_tok_pos, L0_attn_w_qkv, L0_attn_w_proj, L0_attn_b_proj, L0_ffn_f_know,
           L0_ffn_r_know, L0_ffn_W_fk, L0_ffn_b_fk, L0_ffn_W_rk, L0_ffn_b_rk, L0_ffn_emb_fk, L0_ffn_emb_rk):
    import numpy as np
    import concourse.bacc as bacc
    from concourse.bass_utils import run_bass_kernel_spmd as run

    a = np.asarray
    nimg = NT * IMGS
    p = a(x).reshape(B, 3, 4, 16, 4, 16).transpose(0, 2, 4, 1, 3, 5).reshape(B, 16, 768)
    xt = np.zeros((nimg, NPOS, 768), np.float32)
    xt[:B, 1:] = p
    xt = xt.reshape(NT, P, KC, 128).transpose(0, 3, 2, 1)

    def halves(w):
        return w.reshape(2, HC, -1).transpose(1, 0, 2)

    bias = np.zeros((IMGS, NPOS, 2, D), np.float32)
    bias[:, 0, 0] = a(cls_tok).reshape(1, D)
    bias[:, 1:, 0] = a(L0_tok_pos).reshape(1, 16, D)
    bias[:, 1:, 1] = a(L0_tok_b)
    arrays = {
        "xt": xt,
        "wt": a(L0_tok_W).T.reshape(KC, 128, D).transpose(1, 0, 2),
        "bias": bias.reshape(P, 2, D),
        "wqkv": halves(a(L0_attn_w_qkv).T),
        "wproj": halves(a(L0_attn_w_proj).T),
        "bproj": np.broadcast_to(a(L0_attn_b_proj), (P, D)),
        "wmid": halves(np.concatenate([a(L0_ffn_W_fk), a(L0_ffn_W_rk)], axis=1)),
        "bmid": np.concatenate([a(L0_ffn_b_fk), a(L0_ffn_b_rk)]).reshape(128, 1),
        "emb": np.concatenate([a(L0_ffn_emb_fk), a(L0_ffn_emb_rk)], axis=1),
        "fknow": a(L0_ffn_f_know).reshape(NN, 2, HC, R).transpose(2, 0, 1, 3).reshape(HC, NN * 2 * R),
        "rknow": a(L0_ffn_r_know).transpose(1, 0, 2).reshape(R, NN * D),
        "const": constants(np),
    }
    arrays = {k: np.ascontiguousarray(v) for k, v in arrays.items()}
    nc = bacc.Bacc("TRN2", target_bir_lowering=False, num_devices=1)
    args = [nc.dram_tensor(k, v.shape, mybir.dt.from_np(v.dtype), kind="ExternalInput").ap() for k, v in arrays.items()]
    out = nc.dram_tensor("out", [NT, P, D], mybir.dt.float32, kind="ExternalOutput").ap()
    vit_block(nc, *args, out)
    got = run(nc, [arrays], core_ids=[0]).results[0]["out"]
    return np.asarray(got).reshape(nimg, NPOS, D)[:B]
```

```python
import concourse.bass as bass
from concourse import mybir
from contextlib import ExitStack

B, NPOS, D = 128, 17, 192
IMGS = 7
P = IMGS * NPOS
NT = -(-B // IMGS)
KC = 6
HC = D // 2
NH, DH = 12, 16
NN, R, DS, K = 128, 128, 64, 4
BS = 64
NBLK = -(-(NT * P * K // BS + NN) // 8) * 8
ITS = NBLK // 8
ROWS = NBLK * BS
MAXB = -(-NT * P // BS)
CI, CM, CO, CU, CE, CB, CT, CP, CN, CG = 0, 128, 247, 375, 503, 505, 505 + NBLK, 505 + NBLK + MAXB, 506 + NBLK + MAXB, 634 + NBLK + MAXB
NC = CG + 96


def constants(np):
    c = np.zeros((128, NC), np.float32)
    p = np.arange(128)
    c[:, CI:CI + 128] = np.eye(128)
    c[:, CM:CM + P] = (p[:, None] // NPOS) == (np.arange(P)[None] // NPOS)
    c[:, CO:CO + 128] = p[None]
    c[:, CU:CU + 128] = p[:, None] < p[None]
    c[:, CE] = (p // DH) % 2 == 0
    c[:, CE + 1] = (p // DH) % 2 == 1
    c[:, CB:CB + NBLK] = np.arange(NBLK)[None]
    c[:, CT:CT + MAXB] = BS * np.arange(MAXB)[None]
    c[:, CP] = ROWS + p
    c[:, CN:CN + 128] = p[:, None] <= p[None]
    c[:, CG:CG + 96] = (p[:, None] // DH) == (np.arange(96)[None] // DH)
    return c


def vit_block(nc, xt_d, wt_d, bias_d, wqkv_d, wproj_d, bproj_d, wmid_d, bmid_d, emb_d, f_d, r_d, const_d, out_d):
    f32, bf16, i32, u32 = mybir.dt.float32, mybir.dt.bfloat16, mybir.dt.int32, mybir.dt.uint32
    ALU, ACT, AX = mybir.AluOpType, mybir.ActivationFunctionType, mybir.AxisListType
    ds = bass.ds
    ctx = ExitStack()
    with ctx:
        def sb(name, shape, dt=f32):
            return ctx.enter_context(nc.sbuf_tensor(name, shape, dt))

        def ps(name):
            return ctx.enter_context(nc.psum_tensor(name, [128, 512], f32))

        def sem(name):
            return ctx.enter_context(nc.semaphore(name))

        xs_d = nc.dram_tensor("xs", [ROWS, D], f32, kind="Internal").ap()
        ys_d = nc.dram_tensor("ys", [ROWS, R], f32, kind="Internal").ap()
        hs_d = nc.dram_tensor("hs", [ROWS, R], f32, kind="Internal").ap()
        zs_d = nc.dram_tensor("zs", [ROWS, D], f32, kind="Internal").ap()

        W = sb("W", [128, NN * 2 * R])
        CST = sb("CST", [128, NC])
        H = sb("H", [P, NT, D])
        X2W = sb("X2W", [128, NT * D])
        X2 = X2W[0:P].rearrange("p (t d) -> p t d", d=D)
        XBT = X2W[:, 0:2048].rearrange("p (g c) -> p g c", g=4)
        M = sb("M", [P, NT, 2 * NN], bf16)
        MWORK = sb("MWORK", [128, (NT + 1) * NN])
        MPRE = MWORK[0:P, :].bitcast(bf16).rearrange("p (t n) -> p t n", n=2 * NN)
        XB = MWORK[:, 0:8 * D].rearrange("p (j a d) -> p j a d", j=2, a=4)
        TOPA = sb("TOPA", [P, NT, 2, K])
        IDXF = sb("IDXF", [P, NT, 2 * K])
        ZS = sb("ZS", [P, NT, 2])
        WTS = sb("WTS", [P, NT, 2, K])
        WSUM = sb("WSUM", [P, NT, 2])
        SLOTS = sb("SLOTS", [P, NT, 2 * K], i32)
        BASE = sb("BASE", [P, 2 * NN])
        RB = sb("RB", [P, 2 * NN])
        SLF = sb("SLF", [P, 2 * K])
        IDST = sb("IDST", [128, 2, K], i32)
        IDS2 = sb("IDS2", [128, 2, K], i32)
        XSTG = sb("XSTG", [128, 2, D])
        G = sb("G", [128, 2, K, D])
        ZERO = G[:].rearrange("p j k d -> p (j k d)")
        YB = [t[0:BS].rearrange("p (b d) -> p b d", d=D) for t in (G[:].rearrange("p j k d -> p (j k d)"), X2W[:, 2048:2048 + 8 * D])]
        JUNK = G[0:P].rearrange("p j k d -> p (j k d)")[:, 0:2 * K * NN].rearrange("p (k n) -> p k n", n=NN)
        NB = sb("NB", [128, 2], bf16)
        NBF = sb("NBF", [128, 2])
        NBR = sb("NBR", [128, 2, 128], bf16)
        END = sb("END", [128, 2])
        GE = sb("GE", [128, 2, NBLK], bf16)
        ETF = sb("ETF", [1, 2, NBLK])
        ETAB = sb("ETAB", [1, 2, NBLK], i32)
        UB = sb("UB", [128, 128], bf16)
        UIB = sb("UIB", [128, 128], bf16)
        ONES = sb("ONES", [128, 128], bf16)
        THR = sb("THR", [128, MAXB])
        TICK = sb("TICK", [128, 5])

        used = [NN * R]

        def front(parts, shape, dt=f32):
            n = 1
            for s in shape:
                n *= s
            words = (n + 1) // 2 if dt == bf16 else n
            a = W[0:parts, used[0]:used[0] + words]
            used[0] += words + words % 2
            assert used[0] <= NN * 2 * R
            if dt != f32:
                a = a.bitcast(dt)
            names = "abcde"[:len(shape)]
            if len(shape) > 1:
                a = a.rearrange(f"p ({' '.join(names)}) -> p {' '.join(names)}", **dict(zip(names[1:], shape[1:])))
            return a

        XT = front(128, [2, KC, P])
        WT = front(128, [KC, D])
        WQKV = front(HC, [2, 3 * D])
        WPROJ = front(HC, [2, D])
        WMID = front(HC, [2, 2 * DS])
        BMID = front(128, [2])
        EMB = front(128, [2 * DS])
        ESQ = front(128, [2 * DS])
        ENS = front(128, [6, 2])
        EBD = front(128, [2 * NN])
        BIASE = front(P, [2, D])
        BPROJ = front(P, [D])
        LNC = front(P, [4])
        Y = front(P, [2, D])
        X2P = front(P, [2, D])
        YT = front(HC, [2, 2, P])
        Q = front(HC, [2, 2, 2, P])
        KT = front(HC, [2, 2, P])
        EX = front(HC, [4, P])
        RX = front(HC, [6, P])
        V32 = front(P, [2, NH, 2 * DH])
        KS = front(HC, [2, IMGS])
        QKS = front(HC, [2, P])
        SM = front(P, [3, 2, 2, P])
        RD = front(HC, [2, P])
        OT = front(HC, [2, 2, P])
        X2T = front(HC, [2, 2, P])
        MID = front(128, [2, P])
        L = front(P, [2, 2 * NN])
        EJ = front(P, [2, NN])
        ST = front(P, [2, 6])
        MV = front(P, [4, 2])
        RS = front(P, [4, 6])
        TOPP = front(P, [2, 2, 8])
        IDXP = front(P, [2, 2, 8], u32)
        IDXS = front(P, [2, 2 * K])
        NM = front(P, [2, 2])
        MP = front(P, [2, NN], bf16)

        ID = CST[:, CI:CI + 128]
        IMASK = CST[0:P, CM:CM + P]
        IOTA = CST[0:P, CO:CO + NN]

        PB = [ps(f"PB{i}") for i in range(8)]
        PE_PROJ, PE_MID, PE_E = PB[0][0:P, 0:D], PB[1][:, 0:P], PB[4][0:P, 0:D]
        PE_YT = PB[3][0:HC, 0:2 * P].rearrange("p (c t) -> p c t", c=2)
        PE_X2T = PB[3][0:HC, 2 * P:4 * P].rearrange("p (c t) -> p c t", c=2)
        PE_QK = PB[2][0:HC, 0:4 * P].rearrange("p (c t) -> p c t", c=4)
        PE_S = [PB[3 + r][0:P, 0:4 * P].rearrange("p (c e t) -> p c e t", c=2, e=2) for r in range(3)]
        PE_V = PB[6][0:P, 0:D]
        PE_O = PB[6][0:HC, 0:2 * P].rearrange("p (c t) -> p c t", c=2)
        PE_DEN = PB[5][0:HC, 0:2 * P].rearrange("p (c t) -> p c t", c=2)
        PE_L = PB[7][0:P, 0:2 * NN]

        names = """met0 met1 met2 met3 loaded consts_in zeros_set misc_set eb_sq eb_sum eb_sqrt eb_n1 eb_n2 eb_n3 eb_n4 eb_n5 eb_norm eb_T eb_ready
            x_in0 x_in1 emb_done emb_evac st1 stats1 rs1a rs1b rs1c rs1d rs1e rs1f rstd1 y_ready yT_done yT_evac qk_done act_qk qk_ready
            v_done v_ready s_done s_masked o_done o_rec oT_ready ks_ready qsum qks_ready pick0 pick1 hb_ready proj_done h2_ready st2 stats2
            rs2a rs2b rs2c rs2d rs2e rs2f rstd2 x2_ready x2_kept x2T_done x2T_evac mid_done mid_evac log_done log_evac max_done idx_done
            topk_done idx_kept negmax z_done m_ready mpre_ready
            zeroed f_in f_in_upper r_in cnt_done nb_cmp nb_ready nbr_ready base_done base_ready end_ready ge_ready etab_done etf_ready etab_ready
            w1 w2 w3 w4 w5 w6 weights_ready
            rank_done rb_ready slf_ready slots_ready idst_ready xstg_ready
            scat0 scat1 gidx_ready gath0 gath1 comb1 comb2 comb3 hstg_ready ridx_ready rscat0 rscat1
            g2idx_ready g2a0 g2a1 comb21 comb22 comb23 comb24 out_ready out_stored""".split()
        S = {n: sem(n) for n in names}

        class Stage:
            def __init__(self, n):
                self.rows_in = [sem(f"{n}_rows_in{i}") for i in range(2)]
                self.rows_T, self.rows_T_evac = sem(f"{n}_rows_T"), sem(f"{n}_rows_T_evac")
                self.mm_done, self.mm_evac = sem(f"{n}_mm_done"), sem(f"{n}_mm_evac")
                self.stored = [sem(f"{n}_stored{i}") for i in range(2)]

        FEAT, REST = Stage("feat"), Stage("rest")
        block = ctx.enter_context(nc.Block())

        def need(eng, s, val):
            if not isinstance(val, int) or val > 0:
                eng.wait_ge(S[s] if isinstance(s, str) else s, val)

        def apart(eng):
            eng.wait_ge(S["consts_in"], 16)

        def tile_loop(eng, body, first, last, head, tail):
            assert (last + 1 - tail - first - head) % 2 == 0 and (first + head) % 2 == 0
            for i in range(first, first + head):
                body(i, i % 2)
            with eng.Fori(0, (last + 1 - tail - first - head) // 2) as u:
                body(u * 2 + (first + head), 0)
                body(u * 2 + (first + head + 1), 1)
            for i in range(last + 1 - tail, last + 1):
                body(i, i % 2)

        def front_loop(eng, body):
            tile_loop(eng, body, 0, NT + 2, 4, 4)

        def on(i, s):
            return not isinstance(i, int) or 0 <= i - s < NT

        def pair_sem(i, j):
            return 8 * (i - j) + 16

        @block.sync
        def _(sp):
            sp.dma_start(CST[:], const_d).then_inc(S["consts_in"], 16)
            for dst, src in ((WT, wt_d), (BIASE, bias_d), (WQKV, wqkv_d), (EMB, emb_d),
                             (BMID[:, 0:1], bmid_d), (WPROJ, wproj_d), (BPROJ, bproj_d), (WMID, wmid_d)):
                sp.dma_start(dst, src).then_inc(S["loaded"], 16)

            def load_x(i, j):
                need(sp, "emb_done", i - 1)
                sp.dma_start(XT[:, j], xt_d[ds(i, 1)].rearrange("a p c t -> (a p) c t")).then_inc(S[f"x_in{j}"], 16)

            tile_loop(sp, load_x, 0, NT - 1, 2, 1)

            sp.wait_ge(S["m_ready"], NT)
            sp.wait_ge(S["z_done"], NT)
            sp.wait_ge(S["x2_kept"], NT)
            sp.wait_ge(S["idx_kept"], NT)
            sp.wait_ge(S["negmax"], NT)
            for q in (2, 3):
                sp.dma_start(W[0:HC, q * 8192:(q + 1) * 8192], f_d[:, q * 8192:(q + 1) * 8192]).then_inc(S["f_in_upper"], 16)

            def experts(st, src, dst, n):
                def load(i, j):
                    sp.dma_start(XB[:, j, :, 0:n[0]], src[ds(i * 8 * BS, 8 * BS)].rearrange("(a p) d -> p a d", p=128)).then_inc(st.rows_in[j], 16)

                load(0, 0)
                load(1, 1)

                def step(i, j):
                    if not isinstance(i, int) or i + 2 < ITS:
                        need(sp, st.rows_T, 2 * i + 2)
                        load(i + 2, j)
                    need(sp, st.mm_evac, 2 * i + 2)
                    sp.dma_start(dst[ds(i * 8 * BS, 8 * BS)].rearrange("(b p) d -> p b d", p=BS),
                                 YB[j][:, :, 0:n[1]]).then_inc(st.stored[j], 16)
                tile_loop(sp, step, 0, ITS - 1, 2, 2)

            sp.wait_ge(S["scat0"], 64 * ((NT + 1) // 2))
            sp.wait_ge(S["scat1"], 64 * (NT // 2))
            experts(FEAT, xs_d, ys_d, (D, R))
            sp.wait_ge(FEAT.mm_done, 2 * ITS)
            for q in range(4):
                sp.dma_start(W[:, q * 6144:(q + 1) * 6144], r_d[:, q * 6144:(q + 1) * 6144]).then_inc(S["r_in"], 16)
            sp.wait_ge(S["rscat0"], 64 * ((NT + 1) // 2))
            sp.wait_ge(S["rscat1"], 64 * (NT // 2))
            experts(REST, hs_d, zs_d, (R, D))

            def store(i, j):
                need(sp, "out_ready", i + 1)
                sp.dma_start(out_d[ds(i, 1)].rearrange("a t d -> (a t) d"),
                             H[:, ds(i, 1)].rearrange("p a d -> p (a d)")).then_inc(S["out_stored"], 16)
            tile_loop(sp, store, 0, NT - 1, 2, 1)
            sp.wait_ge(S["out_stored"], 16 * NT)

        @block.tensor
        def _(pe):
            mm, tr = nc.tensor.matmul, nc.tensor.transpose
            pe.wait_ge(S["consts_in"], 16)
            pe.wait_ge(S["loaded"], 8 * 16)
            pe.wait_ge(S["eb_norm"], 1)
            tr(PB[7][:, 0:128], ESQ, ID).then_inc(S["eb_T"], 1)

            def step(i, j):
                a, b, c, ja, jb, jc = i - 1, i - 2, i - 3, 1 - j, j, 1 - j
                if on(i, 3):
                    need(pe, "x2_ready", c + 1)
                    if on(i, 2):
                        need(pe, "s_masked", 3 * b + 1)
                    for cc in range(2):
                        last = tr(PE_X2T[:, cc], X2P[:, jc, cc * HC:(cc + 1) * HC], ID[0:P, 0:P])
                    last.then_inc(S["x2T_done"], 1)
                if on(i, 1):
                    need(pe, "y_ready", a + 1)
                    need(pe, "s_masked", 3 * (a - 1) + 1)
                    for cc in range(2):
                        last = tr(PE_YT[:, cc], Y[:, ja, cc * HC:(cc + 1) * HC], ID[0:P, 0:P])
                    last.then_inc(S["yT_done"], 1)
                if on(i, 2):
                    need(pe, "v_ready", b + 1)
                    for r in range(3):
                        need(pe, "s_masked", 3 * b + r + 1)
                        for cc in range(2):
                            for e in range(2):
                                mm(PE_O[32 * r:32 * r + 32, cc], V32[:, jb, 6 * cc + 2 * r + e], SM[:, r, cc, e],
                                   start=(e == 0), stop=(e == 1))
                    need(pe, "qks_ready", b + 1)
                    for cc in range(2):
                        last = mm(PE_DEN[:, cc], CST[0:HC, CG:CG + HC], QKS[:, cc], start=True, stop=True)
                    last.then_inc(S["o_done"], 1)
                if on(i, 1):
                    need(pe, "yT_evac", a + 1)
                    need(pe, "act_qk", a)
                    for m in range(4):
                        for cc in range(2):
                            last = mm(PE_QK[:, m], WQKV[:, cc, m * HC:(m + 1) * HC], YT[:, ja, cc], start=(cc == 0), stop=(cc == 1))
                    last.then_inc(S["qk_done"], 1)
                if on(i, 0):
                    need(pe, S[f"x_in{j}"], pair_sem(i, j))
                    need(pe, "s_masked", 3 * (i - 2) + 2)
                    for k in range(KC):
                        last = mm(PE_E, XT[:, j, k], WT[:, k], start=(k == 0), stop=(k == KC - 1))
                    last.then_inc(S["emb_done"], 1)
                if on(i, 3):
                    need(pe, "x2T_evac", c + 1)
                    need(pe, "mid_evac", c)
                    for cc in range(2):
                        last = mm(PE_MID, WMID[:, cc], X2T[:, jc, cc], start=(cc == 0), stop=(cc == 1))
                    last.then_inc(S["mid_done"], 1)
                if on(i, 1):
                    need(pe, "v_ready", a)
                    need(pe, "oT_ready", a)
                    for cc in range(2):
                        last = mm(PE_V, YT[:, ja, cc], WQKV[:, cc, 2 * D:3 * D], start=(cc == 0), stop=(cc == 1))
                    last.then_inc(S["v_done"], 1)
                if on(i, 2):
                    need(pe, "oT_ready", b + 1)
                    need(pe, "h2_ready", b)
                    for cc in range(2):
                        last = mm(PE_PROJ, OT[:, jb, cc], WPROJ[:, cc], start=(cc == 0), stop=(cc == 1))
                    last.then_inc(S["proj_done"], 1)
                if on(i, 3):
                    need(pe, "mid_evac", c + 1)
                    need(pe, "log_evac", c)
                    if isinstance(c, int) and c == 0:
                        pe.wait_ge(S["eb_ready"], 1)
                    mm(PE_L, MID[:, jc], EBD, start=True, stop=True).then_inc(S["log_done"], 1)
                if on(i, 1):
                    need(pe, "qk_ready", a + 1)
                    if on(i, 0):
                        need(pe, "emb_evac", i + 1)
                    for r in range(3):
                        if r == 2:
                            need(pe, "oT_ready", a)
                        for cc in range(2):
                            last = mm(PE_S[r][:, cc], KT[32 * r:32 * r + 32, ja, cc], Q[32 * r:32 * r + 32, ja, cc], start=True, stop=True)
                        last.then_inc(S["s_done"], 1)

            front_loop(pe, step)

            pe.wait_ge(S["mpre_ready"], NT)
            pe.wait_ge(S["misc_set"], 1)
            for q in range(2):
                last = mm(PB[0][:, q:q + 1], MPRE[:, NT, q * NN:(q + 1) * NN], ONES[0:P, 0:1], start=True, stop=True)
            last.then_inc(S["cnt_done"], 1)
            pe.wait_ge(S["nbr_ready"], 1)
            for q in range(2):
                mm(PB[1][0:P, q * NN:(q + 1) * NN], NBR[:, q, 0:P], UB[:], start=True, stop=True)
            mm(PB[0][:, 2:4], UIB[:], NB[:], start=True, stop=True).then_inc(S["base_done"], 1)
            pe.wait_ge(S["ge_ready"], 1)
            for q in range(2):
                last = mm(PB[6 + q][0:1, 0:NBLK], ONES[:, 0:1], GE[:, q], start=True, stop=True)
            last.then_inc(S["etab_done"], 1)

            def rank(i, j):
                need(pe, "rb_ready", i)
                mm(PB[2][0:P, 0:2 * NN], UB[0:P, 0:P], M[:, ds(i, 1)].rearrange("p a n -> p (a n)"), start=True, stop=False)
                mm(PB[2][0:P, 0:2 * NN], ONES[0:P, 0:P], MPRE[:, ds(i, 1)].rearrange("p a n -> p (a n)"),
                   start=False, stop=True).then_inc(S["rank_done"], 1)
            tile_loop(pe, rank, 0, NT - 1, 2, 1)

            def experts(st, q, na, m, n, wcol):
                def turn(i, j, h):
                    if h == 0:
                        need(pe, st.rows_in[j], pair_sem(i, j))
                    need(pe, st.rows_T_evac, 2 * i + h - 3)
                    for a in range(2):
                        for cc in range(na):
                            t = a * na + cc
                            last = tr(PB[2 * j + h][0:m, t * 128:(t + 1) * 128], XB[:, j, 2 * h + a, cc * m:(cc + 1) * m], ID)
                    last.then_inc(st.rows_T, 1)

                def product(i, j, h):
                    _, e = nc.values_load_multi_w_load_instructions(ETAB[0:1, q, ds(i * 8 + 4 * h, 4)], engines=[mybir.EngineType.PE],
                                                                    min_val=0, max_val=(NN - 1) * wcol,
                                                                    skip_runtime_bounds_check_because="ETAB is clamped to the last neuron")
                    need(pe, st.rows_T_evac, 2 * i + h + 1)
                    need(pe, st.mm_evac, 2 * i + h - 1)
                    for b in range(4):
                        o = PB[4 + 2 * h + b // 2][0:BS, (b % 2) * n:(b % 2) * n + n]
                        for cc in range(na):
                            col = ((b // 2) * na + cc) * 128 + (b % 2) * BS
                            last = mm(o, XBT[0:m, 2 * j + h, col:col + BS], W[0:m, ds(e[b] + cc * n, n)], start=(cc == 0), stop=(cc == na - 1))
                    last.then_inc(st.mm_done, 1)

                turn(0, 0, 0)

                def step(i, j):
                    turn(i, j, 1)
                    product(i, j, 0)
                    if not isinstance(i, int) or i + 1 < ITS:
                        turn(i + 1, 1 - j, 0)
                    product(i, j, 1)
                tile_loop(pe, step, 0, ITS - 1, 2, 2)

            pe.wait_ge(S["etab_ready"], 1)
            pe.wait_ge(S["f_in"], 32)
            pe.wait_ge(S["f_in_upper"], 32)
            experts(FEAT, 0, 2, HC, R, 2 * R)
            pe.wait_ge(S["r_in"], 64)
            experts(REST, 1, 1, 128, D, D)

        @block.scalar
        def _(act):
            A = nc.scalar.activation
            act.wait_ge(S["consts_in"], 16)
            act.wait_ge(S["loaded"], 8 * 16)
            act.wait_ge(S["eb_sum"], 1)
            A(ENS[:, 1], ENS[:, 0], ACT.Sqrt).then_inc(S["eb_sqrt"], 1)

            def step(i, j):
                a, b, c, ja, jb, jc = i - 1, i - 2, i - 3, 1 - j, j, 1 - j
                if on(i, 3):
                    need(act, "x2T_done", c + 1)
                    if on(i, 1):
                        need(act, "yT_done", a + 1)
                    need(act, "mid_done", c - 1)
                    nc.scalar.copy(X2T[:, jc], PE_X2T).then_inc(S["x2T_evac"], 1)
                if on(i, 1):
                    need(act, "yT_done", a + 1)
                    need(act, "v_done", a - 1)
                    nc.scalar.copy(YT[:, ja], PE_YT).then_inc(S["yT_evac"], 1)
                if on(i, 1):
                    need(act, "qk_done", a + 1)
                    need(act, "qk_ready", a)
                    A(EX, PE_QK, ACT.Exp)
                    A(RX[:, 0:2], PE_QK[:, 0:2], ACT.Relu, scale=CST[0:HC, CE:CE + 1])
                    A(RX[:, 2:4], PE_QK[:, 0:2], ACT.Relu, scale=CST[0:HC, CE + 1:CE + 2])
                    A(RX[:, 4:6], PE_QK[:, 2:4], ACT.Relu).then_inc(S["act_qk"], 1)
                if on(i, 3):
                    need(act, "mid_done", c + 1)
                    need(act, "log_done", c - 1)
                    A(MID[:, jc], PE_MID, ACT.Identity, bias=BMID[:, 0:1]).then_inc(S["mid_evac"], 1)
                if on(i, 1):
                    need(act, "v_done", a + 1)
                    need(act, "o_done", a - 1)
                    if isinstance(a, int) and a == 0:
                        act.wait_ge(S["misc_set"], 1)
                    v32 = V32[:, ja].rearrange("p (h e) d -> p h e d", e=2)
                    v = PE_V.rearrange("p (h e d) -> p h e d", e=2, d=DH)
                    nc.scalar.copy(v32[:, :, 0, 0:DH], v[:, :, 0])
                    nc.scalar.copy(v32[:, :, 1, DH:2 * DH], v[:, :, 1]).then_inc(S["v_ready"], 1)
                if on(i, 3):
                    need(act, "log_done", c + 1)
                    need(act, "idx_done", c - 1)
                    nc.scalar.copy(L[:, jc], PE_L).then_inc(S["log_evac"], 1)
                    need(act, "negmax", c + 1)
                    need(act, "z_done", c)
                    for q in range(2):
                        last = A(EJ[:, q], L[:, jc, q * NN:(q + 1) * NN], ACT.Exp, bias=NM[:, jc, q:q + 1],
                                 accum_out=ZS[:, ds(c, 1), q:q + 1].rearrange("p a q -> p (a q)"))
                    last.then_inc(S["z_done"], 1)

            front_loop(act, step)

            def stage_x(i, j):
                if not isinstance(i, int) or i >= 2:
                    act.wait_ge(S[f"scat{j}"], 32 * (i - j))
                else:
                    act.wait_ge(S["misc_set"], 1)
                nc.scalar.copy(XSTG[0:P, j], X2[:, ds(i, 1)].rearrange("p a d -> p (a d)")).then_inc(S["xstg_ready"], 1)
            tile_loop(act, stage_x, 0, NT - 1, 2, 1)
            act.wait_ge(S["w1"], 1)
            A(WTS[:], WTS[:], ACT.Exp).then_inc(S["w2"], 1)

            def experts(st, m, w):
                def step(i, j):
                    for h in range(2):
                        need(act, st.rows_T, 2 * i + h + 1)
                        need(act, st.mm_done, 2 * i + h - 3)
                        nc.scalar.copy(XBT[0:m, 2 * j + h, 0:w], PB[2 * j + h][0:m, 0:w]).then_inc(st.rows_T_evac, 1)
                tile_loop(act, step, 0, ITS - 1, 2, 2)
            experts(FEAT, HC, 512)
            experts(REST, 128, 256)

        @block.vector
        def _(dve):
            V = nc.vector
            V.memset(ZERO[:], 0.0).then_inc(S["zeros_set"], 1)
            V.memset(ONES[:], 1.0)
            V.memset(LNC[:, 0:1], -0.5)
            V.memset(LNC[:, 1:2], 1e-5)
            V.memset(LNC[:, 2:3], 1.5)
            V.memset(XSTG[:], 0.0)
            V.memset(TICK[:], 0.0)
            V.memset(V32, 0.0)
            V.memset(MPRE[:, 0], 0.0)
            dve.wait_ge(S["loaded"], 8 * 16)
            dve.wait_ge(S["consts_in"], 16)
            V.tensor_copy(UB[:], CST[:, CU:CU + 128])
            V.tensor_copy(UIB[:], CST[:, CN:CN + 128])
            for q in range(2):
                for k in range(K):
                    V.tensor_copy(IDST[:, q, k:k + 1], CST[:, CP:CP + 1])
                    V.tensor_copy(IDS2[:, q, k:k + 1], CST[:, CP:CP + 1])
            V.memset(EBD, 0.0)
            V.tensor_tensor(BIASE[:, 0], BIASE[:, 0], BIASE[:, 1], ALU.add).then_inc(S["misc_set"], 1)
            V.tensor_tensor(ESQ, EMB, EMB, ALU.mult).then_inc(S["eb_sq"], 1)
            dve.wait_ge(S["eb_sq"], 1)
            V.tensor_reduce(ENS[:, 0], ESQ.rearrange("p (q d) -> p q d", q=2), axis=AX.X, op=ALU.add).then_inc(S["eb_sum"], 1)
            dve.wait_ge(S["eb_sqrt"], 1)
            V.tensor_scalar(ENS[:, 2], ENS[:, 1], 1e-30, None, ALU.max).then_inc(S["eb_n1"], 1)
            dve.wait_ge(S["eb_n1"], 1)
            V.reciprocal(ENS[:, 3], ENS[:, 2]).then_inc(S["eb_n2"], 1)
            dve.wait_ge(S["eb_n2"], 1)
            V.tensor_tensor(ENS[:, 3], ENS[:, 3], ENS[:, 0], ALU.mult).then_inc(S["eb_n3"], 1)
            dve.wait_ge(S["eb_n3"], 1)
            V.tensor_tensor(ENS[:, 3], ENS[:, 3], ENS[:, 1], ALU.add).then_inc(S["eb_n4"], 1)
            dve.wait_ge(S["eb_n4"], 1)
            V.tensor_scalar(ENS[:, 4], ENS[:, 3], 0.5, 1e-8, ALU.mult, ALU.add).then_inc(S["eb_n5"], 1)
            dve.wait_ge(S["eb_n5"], 1)
            V.reciprocal(ENS[:, 5], ENS[:, 4]).then_inc(S["eb_n5"], 1)
            dve.wait_ge(S["eb_n5"], 2)
            V.tensor_tensor(ESQ.rearrange("p (q d) -> p q d", q=2), EMB.rearrange("p (q d) -> p q d", q=2),
                            ENS[:, 5].rearrange("p (q o) -> p q o", o=1).broadcast_to([128, 2, DS]), ALU.mult).then_inc(S["eb_norm"], 1)
            dve.wait_ge(S["eb_T"], 1)
            V.tensor_copy(EBD[0:DS, 0:NN], PB[7][0:DS, 0:NN])
            V.tensor_copy(EBD[DS:128, NN:2 * NN], PB[7][DS:128, 0:NN]).then_inc(S["eb_ready"], 1)
            dve.wait_ge(S["misc_set"], 1)

            def row(buf, t):
                return buf[:, ds(t, 1)].rearrange("p a d -> p (a d)")

            def step(i, j):
                a, b, c, ja, jb, jc = i - 1, i - 2, i - 3, 1 - j, j, 1 - j
                if on(i, 2):
                    need(dve, "o_done", b + 1)
                    V.reciprocal(RD, PE_DEN).then_inc(S["o_rec"], 1)
                    need(dve, "o_rec", b + 1)
                    need(dve, "proj_done", b - 1)
                    V.tensor_tensor(OT[:, jb], PE_O, RD, ALU.mult).then_inc(S["oT_ready"], 1)
                if on(i, 1):
                    need(dve, "act_qk", a + 1)
                    for e in range(2):
                        V.scalar_tensor_tensor(Q[:, ja, :, e], EX[:, 0:2], CST[0:HC, CE + e:CE + e + 1], RX[:, 2 * e:2 * e + 2],
                                               ALU.min, ALU.add)
                    V.scalar_tensor_tensor(KT[:, ja], EX[:, 2:4], 1.0, RX[:, 4:6], ALU.min, ALU.add).then_inc(S["qk_ready"], 1)
                if on(i, 0):
                    need(dve, "emb_done", i + 1)
                    V.tensor_tensor(row(H, i), PE_E, BIASE[:, 0], ALU.add).then_inc(S["emb_evac"], 1)
                    apart(dve)
                    need(dve, "emb_evac", i + 1)
                    apart(dve)
                    V.bn_stats(ST[:, 0], row(H, i)).then_inc(S["st1"], 1)
                if on(i, 1):
                    need(dve, "qk_ready", a + 1)
                    need(dve, "qks_ready", a)
                    V.tensor_reduce(KS, KT[:, ja].rearrange("p c (m t) -> p c m t", m=IMGS), axis=AX.X, op=ALU.add).then_inc(S["ks_ready"], 1)
                if on(i, 0):
                    apart(dve)
                    need(dve, "st1", i + 1)
                    apart(dve)
                    V.bn_aggr(MV[:, j], ST[:, 0]).then_inc(S["stats1"], 1)
                if on(i, 1):
                    need(dve, "o_done", a)
                    V.tensor_tensor(QKS, Q[:, ja, :, 0], Q[:, ja, :, 1], ALU.add).then_inc(S["qsum"], 1)
                    need(dve, "ks_ready", a + 1)
                    need(dve, "qsum", a + 1)
                    q4 = QKS.rearrange("p c (m t) -> p (c m) t", m=IMGS)
                    V.tensor_tensor(q4, q4, KS.rearrange("p c (m o) -> p (c m) o", o=1).broadcast_to([HC, 2 * IMGS, NPOS]),
                                    ALU.mult).then_inc(S["qks_ready"], 1)
                if on(i, 2):
                    need(dve, "proj_done", b + 1)
                    need(dve, "hb_ready", b + 1)
                    V.tensor_tensor(row(H, b), PE_PROJ, row(H, b), ALU.add).then_inc(S["h2_ready"], 1)
                if on(i, 0):
                    need(dve, "rstd1", i + 1)
                    V.tensor_scalar(Y[:, j], row(H, i), MV[:, j, 0:1], RS[:, j, 5:6], ALU.subtract, ALU.mult).then_inc(S["y_ready"], 1)
                if on(i, 2):
                    apart(dve)
                    need(dve, "h2_ready", b + 1)
                    apart(dve)
                    V.bn_stats(ST[:, 1], row(H, b)).then_inc(S["st2"], 1)
                    apart(dve)
                    need(dve, "st2", b + 1)
                    apart(dve)
                    V.bn_aggr(MV[:, 2 + jb], ST[:, 1]).then_inc(S["stats2"], 1)
                if on(i, 3):
                    apart(dve)
                    need(dve, "log_evac", c + 1)
                    apart(dve)
                    for q in range(2):
                        last = V.max(TOPP[:, jc, q], L[:, jc, q * NN:(q + 1) * NN])
                    last.then_inc(S["max_done"], 1)
                if on(i, 1):
                    need(dve, "o_done", a)
                    for r in range(3):
                        need(dve, "s_done", 3 * a + r + 1)
                        V.tensor_tensor(SM[:, r].rearrange("p c e t -> p (c e) t"), PE_S[r].rearrange("p c e t -> p (c e) t"),
                                        IMASK.rearrange("p (o t) -> p o t", o=1).broadcast_to([P, 4, P]), ALU.mult).then_inc(S["s_masked"], 1)
                if on(i, 3):
                    need(dve, "max_done", c + 1)
                    V.tensor_scalar(NM[:, jc], TOPP[:, jc, :, 0], -1.0, None, ALU.mult).then_inc(S["negmax"], 1)
                    for q in range(2):
                        last = V.max_index(IDXP[:, jc, q], TOPP[:, jc, q], L[:, jc, q * NN:(q + 1) * NN])
                    last.then_inc(S["idx_done"], 1)
                    V.tensor_copy(TOPA[:, ds(c, 1)].rearrange("p a q k -> p (a q) k"), TOPP[:, jc, :, 0:K])
                    need(dve, "idx_done", c + 1)
                    need(dve, "idx_kept", c - 1)
                    V.tensor_copy(IDXS[:, jc].rearrange("p (q k) -> p q k", q=2), IDXP[:, jc, :, 0:K]).then_inc(S["topk_done"], 1)
                if on(i, 2):
                    need(dve, "rstd2", b + 1)
                    need(dve, "x2_kept", b - 1)
                    V.tensor_scalar(X2P[:, jb], row(H, b), MV[:, 2 + jb, 0:1], RS[:, 2 + jb, 5:6], ALU.subtract, ALU.mult).then_inc(S["x2_ready"], 1)
                if on(i, 3):
                    need(dve, "topk_done", c + 1)
                    need(dve, "m_ready", c)
                    for k in range(K):
                        for q in range(2):
                            m, at = MP[:, q], IDXS[:, jc, q * K + k:q * K + k + 1]
                            if k == 0:
                                V.tensor_scalar(m, IOTA, at, None, ALU.is_equal).then_inc(S[f"pick{q}"], 1)
                            else:
                                need(dve, f"pick{q}", c * (K - 1) + k)
                                last = V.scalar_tensor_tensor(row(M, c)[:, q * NN:(q + 1) * NN] if k == K - 1 else m,
                                                              IOTA, at, m, ALU.is_equal, ALU.add)
                                if k < K - 1:
                                    last.then_inc(S[f"pick{q}"], 1)
                    last.then_inc(S["m_ready"], 1)

            front_loop(dve, step)

            dve.wait_ge(S["cnt_done"], 1)
            for q in range(2):
                V.tensor_scalar(THR[:], CST[:, CT:CT + MAXB], PB[0][:, q:q + 1], 0.0, ALU.is_lt, ALU.add,
                                accum_out=NBF[:, q:q + 1]).then_inc(S["nb_cmp"], 1)
                dve.wait_ge(S["nb_cmp"], q + 1)
            V.tensor_copy(NB[:], NBF[:]).then_inc(S["nb_ready"], 1)
            for q in range(2):
                last = V.tensor_scalar(NBR[:, q], ONES[:], NBF[:, q:q + 1], None, ALU.mult)
            last.then_inc(S["nbr_ready"], 1)
            dve.wait_ge(S["base_done"], 1)
            V.tensor_scalar(BASE[:], PB[1][0:P, 0:2 * NN], float(BS), None, ALU.mult).then_inc(S["base_ready"], 1)
            V.tensor_copy(END[:], PB[0][:, 2:4]).then_inc(S["end_ready"], 1)
            dve.wait_ge(S["end_ready"], 1)
            for q in range(2):
                last = V.tensor_scalar(GE[:, q], CST[:, CB:CB + NBLK], END[:, q:q + 1], None, ALU.is_ge)
            last.then_inc(S["ge_ready"], 1)
            dve.wait_ge(S["etab_done"], 1)
            for q in range(2):
                last = V.tensor_scalar(ETF[:, q], PB[6 + q][0:1, 0:NBLK], float(NN - 1), float((2 * R, D)[q]), ALU.min, ALU.mult)
            last.then_inc(S["etf_ready"], 1)
            dve.wait_ge(S["etf_ready"], 1)
            V.tensor_copy(ETAB[:], ETF[:]).then_inc(S["etab_ready"], 1)

            def slots(i, j):
                need(dve, "rank_done", i + 1)
                V.tensor_tensor(RB[:], PB[2][0:P, 0:2 * NN], BASE[:], ALU.add).then_inc(S["rb_ready"], 1)
                need(dve, "rb_ready", i + 1)
                for k in range(2 * K):
                    q = k // K
                    last = V.scalar_tensor_tensor(JUNK[:, k], IOTA, IDXF[:, ds(i, 1), k:k + 1].rearrange("p a k -> p (a k)"),
                                                  RB[:, q * NN:(q + 1) * NN], ALU.is_equal, ALU.mult, accum_out=SLF[:, k:k + 1])
                last.then_inc(S["slf_ready"], 1)
                need(dve, "slf_ready", i + 1)
                V.tensor_copy(SLOTS[:, ds(i, 1)].rearrange("p a k -> p (a k)"), SLF[:]).then_inc(S["slots_ready"], 1)
                if not isinstance(i, int) or i >= 2:
                    dve.wait_ge(S[f"scat{j}"], 32 * (i - j))
                V.tensor_copy(IDST[0:P, j], SLF[:, 0:K]).then_inc(S["idst_ready"], 1)
            dve.wait_ge(S["base_ready"], 1)
            dve.wait_ge(S["zeroed"], 32)
            tile_loop(dve, slots, 0, NT - 1, 2, 1)

            dve.wait_ge(S["z_done"], NT)
            V.tensor_tensor(WTS[:], TOPA[:], TOPA[:, :, :, 0:1].broadcast_to([P, NT, 2, K]), ALU.subtract).then_inc(S["w1"], 1)
            V.reciprocal(ZS[:], ZS[:]).then_inc(S["w3"], 1)
            dve.wait_ge(S["w2"], 1)
            dve.wait_ge(S["w3"], 1)

            def over_k(t):
                return t[:].rearrange("p t (q o) -> p t q o", o=1).broadcast_to([P, NT, 2, K])
            V.tensor_tensor(WTS[:], WTS[:], over_k(ZS), ALU.mult).then_inc(S["w4"], 1)
            dve.wait_ge(S["w4"], 1)
            V.tensor_reduce(WSUM[:], WTS[:], axis=AX.X, op=ALU.add).then_inc(S["w5"], 1)
            dve.wait_ge(S["w5"], 1)
            V.tensor_scalar(WSUM[:], WSUM[:], 1e-8, None, ALU.add).then_inc(S["w5"], 1)
            dve.wait_ge(S["w5"], 2)
            V.reciprocal(WSUM[:], WSUM[:]).then_inc(S["w6"], 1)
            dve.wait_ge(S["w6"], 1)
            V.tensor_tensor(WTS[:], WTS[:], over_k(WSUM), ALU.mult).then_inc(S["weights_ready"], 1)

            def experts(st, n):
                def step(i, j):
                    if not isinstance(i, int) or i >= 2:
                        dve.wait_ge(st.stored[j], 8 * (i - j))
                    for h in range(2):
                        need(dve, st.mm_done, 2 * i + h + 1)
                        for u in range(2):
                            last = V.tensor_copy(YB[j][:, 4 * h + 2 * u:4 * h + 2 * u + 2, 0:n],
                                                 PB[4 + 2 * h + u][0:BS, 0:2 * n].rearrange("p (b n) -> p b n", b=2))
                        last.then_inc(st.mm_evac, 1)
                tile_loop(dve, step, 0, ITS - 1, 2, 2)

            experts(FEAT, R)
            dve.wait_ge(S["weights_ready"], 1)

            def idx1(i, j):
                if not isinstance(i, int) or i >= 2:
                    dve.wait_ge(S[f"gath{j}"], 32 * (i - j))
                V.tensor_copy(IDST[0:P, j], SLOTS[:, ds(i, 1), 0:K].rearrange("p a k -> p (a k)")).then_inc(S["gidx_ready"], 1)

            def idx_h(i, j):
                if not isinstance(i, int) or i >= 2:
                    dve.wait_ge(S[f"rscat{j}"], 32 * (i - j))
                V.tensor_copy(IDS2[0:P, j], SLOTS[:, ds(i, 1), K:2 * K].rearrange("p a k -> p (a k)")).then_inc(S["ridx_ready"], 1)

            def weight(i, q, k):
                return WTS[:, ds(i, 1), q, k:k + 1].rearrange("p a k -> p (a k)")

            def combine1(i, j):
                dve.wait_ge(S[f"gath{j}"], 32 * (i - j) + 64)
                g, h = G[0:P, j], XSTG[0:P, j, 0:R]
                V.tensor_scalar(h, g[:, 0, 0:R], weight(i, 0, 0), None, ALU.mult).then_inc(S["comb1"], 1)
                need(dve, "comb1", i + 1)
                V.scalar_tensor_tensor(h, g[:, 1, 0:R], weight(i, 0, 1), h, ALU.mult, ALU.add).then_inc(S["comb2"], 1)
                need(dve, "comb2", i + 1)
                V.scalar_tensor_tensor(h, g[:, 2, 0:R], weight(i, 0, 2), h, ALU.mult, ALU.add).then_inc(S["comb3"], 1)
                need(dve, "comb3", i + 1)
                V.scalar_tensor_tensor(h, g[:, 3, 0:R], weight(i, 0, 3), h, ALU.mult, ALU.add).then_inc(S["hstg_ready"], 1)

            idx1(0, 0)
            idx1(1, 1)

            def middle(i, j):
                idx_h(i, j)
                combine1(i, j)
                if not isinstance(i, int) or i + 2 < NT:
                    idx1(i + 2, j)
            tile_loop(dve, middle, 0, NT - 1, 2, 3)

            experts(REST, D)

            def idx2(i, j):
                if not isinstance(i, int) or i >= 2:
                    dve.wait_ge(S[f"g2a{j}"], 32 * (i - j))
                V.tensor_copy(IDST[0:P, j], SLOTS[:, ds(i, 1), K:2 * K].rearrange("p a k -> p (a k)")).then_inc(S["g2idx_ready"], 1)

            def finish(i, j):
                dve.wait_ge(S[f"g2a{j}"], 32 * (i - j) + 64)
                for k in range(K):
                    last = V.scalar_tensor_tensor(row(H, i), G[0:P, j, k], weight(i, 1, k), row(H, i), ALU.mult, ALU.add)
                    if k < K - 1:
                        last.then_inc(S[f"comb2{k + 1}"], 1)
                        need(dve, f"comb2{k + 1}", i + 1)
                last.then_inc(S["out_ready"], 1)
                if not isinstance(i, int) or i + 2 < NT:
                    idx2(i + 2, j)
            idx2(0, 0)
            idx2(1, 1)
            tile_loop(dve, finish, 0, NT - 1, 2, 3)

        @block.gpsimd
        def _(pool):
            GP = nc.gpsimd
            pool.wait_ge(S["consts_in"], 16)
            pool.wait_ge(S["zeros_set"], 1)
            nz = ROWS // 128 // 8
            for dst, n in ((xs_d, D), (hs_d, R)):
                pool.dma_start(dst[0:ROWS].rearrange("(p s r) d -> p s (r d)", p=128, r=8),
                               ZERO[:, 0:8 * n].rearrange("p (o n) -> p o n", o=1).broadcast_to([128, nz, 8 * n])).then_inc(S["zeroed"], 16)
            for q in (0, 1):
                pool.dma_start(W[0:HC, q * 8192:(q + 1) * 8192], f_d[:, q * 8192:(q + 1) * 8192]).then_inc(S["f_in"], 16)
            pool.wait_ge(S["misc_set"], 1)

            def rstd(m, r, s, t):
                def c(k):
                    return RS[:, r, k:k + 1]
                GP.tensor_tensor(c(0), MV[:, m, 1:2], LNC[:, 1:2], ALU.add).then_inc(S[s + "a"], 1)
                need(pool, s + "a", t + 1)
                GP.tensor_tensor(c(1), c(0), LNC[:, 0:1], ALU.pow).then_inc(S[s + "b"], 1)
                need(pool, s + "b", t + 1)
                GP.tensor_tensor(c(2), c(1), c(1), ALU.mult).then_inc(S[s + "c"], 1)
                need(pool, s + "c", t + 1)
                GP.tensor_tensor(c(3), c(2), c(0), ALU.mult).then_inc(S[s + "d"], 1)
                need(pool, s + "d", t + 1)
                GP.tensor_tensor(c(4), c(3), LNC[:, 0:1], ALU.mult).then_inc(S[s + "e"], 1)
                need(pool, s + "e", t + 1)
                GP.tensor_tensor(c(3), c(4), LNC[:, 2:3], ALU.add).then_inc(S[s + "f"], 1)
                need(pool, s + "f", t + 1)
                GP.tensor_tensor(c(5), c(3), c(1), ALU.mult).then_inc(S["rstd" + s[2]], 1)

            def step(i, j):
                a, b, c, ja, jb, jc = i - 1, i - 2, i - 3, 1 - j, j, 1 - j
                if on(i, 0):
                    need(pool, "stats1", i + 1)
                    need(pool, "y_ready", i - 1)
                    rstd(j, j, "rs1", i)
                if on(i, 1):
                    need(pool, "y_ready", a + 1)
                    h = H[:, ds(a, 1)].rearrange("p a d -> p (a d)")
                    GP.tensor_tensor(h, h, BPROJ, ALU.add).then_inc(S["hb_ready"], 1)
                if on(i, 2):
                    need(pool, "stats2", b + 1)
                    need(pool, "x2_ready", b - 1)
                    rstd(2 + jb, 2 + jb, "rs2", b)
                    need(pool, "x2_ready", b + 1)
                    GP.tensor_copy(X2[:, ds(b, 1)].rearrange("p a d -> p (a d)"), X2P[:, jb]).then_inc(S["x2_kept"], 1)
                if on(i, 3):
                    need(pool, "topk_done", c + 1)
                    GP.tensor_copy(IDXF[:, ds(c, 1)].rearrange("p a k -> p (a k)"), IDXS[:, jc]).then_inc(S["idx_kept"], 1)
                    need(pool, "m_ready", c + 1)
                    need(pool, "mpre_ready", c)
                    GP.tensor_tensor(MPRE[:, ds(c + 1, 1)].rearrange("p a n -> p (a n)"), MPRE[:, ds(c, 1)].rearrange("p a n -> p (a n)"),
                                     M[:, ds(c, 1)].rearrange("p a n -> p (a n)"), ALU.add).then_inc(S["mpre_ready"], 1)

            front_loop(pool, step)

            def meet(site, i):
                need(pool, f"met{site}", i)
                GP.tensor_tensor(TICK[:, site:site + 1], TICK[:, 4:5], TICK[:, 4:5], ALU.add).then_inc(S[f"met{site}"], 1)

            def off(ids, j, k):
                return bass.IndirectOffsetOnAxis(ap=ids[:, j, k:k + 1], axis=0)

            pool.wait_ge(S["zeroed"], 32)

            def scatter_x(i, j):
                need(pool, "idst_ready", i + 1)
                need(pool, "xstg_ready", i + 1)
                meet(0, i)
                for k in range(K):
                    pool.indirect_dma_start(out=xs_d, out_offset=off(IDST, j, k), in_=XSTG[:, j], in_offset=None,
                                            bounds_check=ROWS - 1, oob_is_err=False).then_inc(S[f"scat{j}"], 16)
            tile_loop(pool, scatter_x, 0, NT - 1, 2, 1)

            pool.wait_ge(FEAT.stored[0], 16 * (ITS // 2))
            pool.wait_ge(FEAT.stored[1], 16 * (ITS // 2))

            def gather_y(i, j):
                need(pool, "gidx_ready", i + 1)
                need(pool, "hstg_ready", i - 1)
                meet(1, i)
                for k in range(K):
                    pool.indirect_dma_start(out=G[:, j, k, 0:R], out_offset=None, in_=ys_d, in_offset=off(IDST, j, k),
                                            bounds_check=ROWS - 1, oob_is_err=False).then_inc(S[f"gath{j}"], 16)

            gather_y(0, 0)

            def middle(i, j):
                if not isinstance(i, int) or i + 1 < NT:
                    gather_y(i + 1, 1 - j)
                need(pool, "ridx_ready", i + 1)
                need(pool, "hstg_ready", i + 1)
                meet(2, i)
                for k in range(K):
                    pool.indirect_dma_start(out=hs_d, out_offset=off(IDS2, j, k), in_=XSTG[:, j, 0:R], in_offset=None,
                                            bounds_check=ROWS - 1, oob_is_err=False).then_inc(S[f"rscat{j}"], 16)
            tile_loop(pool, middle, 0, NT - 1, 2, 3)

            pool.wait_ge(REST.stored[0], 16 * (ITS // 2))
            pool.wait_ge(REST.stored[1], 16 * (ITS // 2))

            def gather_z(i, j):
                need(pool, "g2idx_ready", i + 1)
                need(pool, "out_ready", i - 1)
                meet(3, i)
                for k in range(K):
                    pool.indirect_dma_start(out=G[:, j, k], out_offset=None, in_=zs_d, in_offset=off(IDST, j, k),
                                            bounds_check=ROWS - 1, oob_is_err=False).then_inc(S[f"g2a{j}"], 16)
            tile_loop(pool, gather_z, 0, NT - 1, 2, 1)


def kernel(x, cls_tok, L0_tok_W, L0_tok_b, L0_tok_pos, L0_attn_w_qkv, L0_attn_w_proj, L0_attn_b_proj, L0_ffn_f_know,
           L0_ffn_r_know, L0_ffn_W_fk, L0_ffn_b_fk, L0_ffn_W_rk, L0_ffn_b_rk, L0_ffn_emb_fk, L0_ffn_emb_rk):
    import numpy as np
    import concourse.bacc as bacc
    from concourse.bass_utils import run_bass_kernel_spmd as run

    a = np.asarray
    nimg = NT * IMGS
    p = a(x).reshape(B, 3, 4, 16, 4, 16).transpose(0, 2, 4, 1, 3, 5).reshape(B, 16, 768)
    xt = np.zeros((nimg, NPOS, 768), np.float32)
    xt[:B, 1:] = p
    xt = xt.reshape(NT, P, KC, 128).transpose(0, 3, 2, 1)

    def halves(w):
        return w.reshape(2, HC, -1).transpose(1, 0, 2)

    bias = np.zeros((IMGS, NPOS, 2, D), np.float32)
    bias[:, 0, 0] = a(cls_tok).reshape(1, D)
    bias[:, 1:, 0] = a(L0_tok_pos).reshape(1, 16, D)
    bias[:, 1:, 1] = a(L0_tok_b)
    arrays = {
        "xt": xt,
        "wt": a(L0_tok_W).T.reshape(KC, 128, D).transpose(1, 0, 2),
        "bias": bias.reshape(P, 2, D),
        "wqkv": halves(a(L0_attn_w_qkv).T),
        "wproj": halves(a(L0_attn_w_proj).T),
        "bproj": np.broadcast_to(a(L0_attn_b_proj), (P, D)),
        "wmid": halves(np.concatenate([a(L0_ffn_W_fk), a(L0_ffn_W_rk)], axis=1)),
        "bmid": np.concatenate([a(L0_ffn_b_fk), a(L0_ffn_b_rk)]).reshape(128, 1),
        "emb": np.concatenate([a(L0_ffn_emb_fk), a(L0_ffn_emb_rk)], axis=1),
        "fknow": a(L0_ffn_f_know).reshape(NN, 2, HC, R).transpose(2, 0, 1, 3).reshape(HC, NN * 2 * R),
        "rknow": a(L0_ffn_r_know).transpose(1, 0, 2).reshape(R, NN * D),
        "const": constants(np),
    }
    arrays = {k: np.ascontiguousarray(v) for k, v in arrays.items()}
    nc = bacc.Bacc("TRN2", target_bir_lowering=False, num_devices=1)
    args = [nc.dram_tensor(k, v.shape, mybir.dt.from_np(v.dtype), kind="ExternalInput").ap() for k, v in arrays.items()]
    out = nc.dram_tensor("out", [NT, P, D], mybir.dt.float32, kind="ExternalOutput").ap()
    vit_block(nc, *args, out)
    got = run(nc, [arrays], core_ids=[0]).results[0]["out"]
    return np.asarray(got).reshape(nimg, NPOS, D)[:B]
```

```python
import concourse.bass as bass
from concourse import mybir
from contextlib import ExitStack

B, NPOS, D = 128, 17, 192
IMGS = 7
P = IMGS * NPOS
NT = -(-B // IMGS)
KC = 6
HC = D // 2
NH, DH = 12, 16
NN, R, DS, K = 128, 128, 64, 4
BS = 64
QT = B * NPOS // 128
NBLK = -(-((B * NPOS * K + NN * (BS - 1)) // BS) // 8) * 8
ITS = NBLK // 8
ROWS = NBLK * BS
HI = ROWS // 128
MAXB = -(-NT * P // BS)
PARTS = NT - 3
FCOLS = NN * R // PARTS
RCOLS = NN * D // PARTS
CI, CM, CO, CU, CE, CB, CT, CN, CG = 0, 128, 247, 375, 503, 505, 505 + NBLK, 505 + NBLK + MAXB, 633 + NBLK + MAXB
CR, CQ, CV = CG + 96, CG + 96 + NT, CG + 96 + 2 * NT
NC = CV + 2
MAGIC = 1.5 * 2 ** 23


def constants(np):
    c = np.zeros((128, NC), np.float32)
    p = np.arange(128)
    c[:, CI:CI + 128] = np.eye(128)
    c[:, CM:CM + P] = (p[:, None] // NPOS) == (np.arange(P)[None] // NPOS)
    c[:, CO:CO + 128] = p[None]
    c[:, CU:CU + 128] = p[:, None] < p[None]
    c[:, CE] = (p // DH) % 2 == 0
    c[:, CE + 1] = (p // DH) % 2 == 1
    c[:, CB:CB + NBLK] = np.arange(NBLK)[None]
    c[:, CT:CT + MAXB] = BS * np.arange(MAXB)[None]
    c[:, CN:CN + 128] = p[:, None] <= p[None]
    c[:, CG:CG + 96] = (p[:, None] // DH) == (np.arange(96)[None] // DH)
    c[:, CR:CR + NT] = np.arange(NT)[None] * P + p[:, None]
    c[:, CR:CR + NT] *= c[:, CR:CR + NT] < B * NPOS
    c[:, CV] = (NT - 1) * P + p < B * NPOS
    c[:, CV + 1] = c[:, CV] - 1
    c[:, CQ:CQ + NT] = -c[:, CR:CR + NT]
    return c


def vit_block(nc, xt_d, wt_d, bias_d, wqkv_d, wproj_d, bproj_d, wmid_d, bmid_d, emb_d, f_d, r_d, const_d, out_d):
    f32, bf16, i32, u32 = mybir.dt.float32, mybir.dt.bfloat16, mybir.dt.int32, mybir.dt.uint32
    ALU, ACT, AX = mybir.AluOpType, mybir.ActivationFunctionType, mybir.AxisListType
    ds = bass.ds
    ctx = ExitStack()
    with ctx:
        def sb(name, shape, dt=f32):
            return ctx.enter_context(nc.sbuf_tensor(name, shape, dt))

        def ps(name):
            return ctx.enter_context(nc.psum_tensor(name, [128, 512], f32))

        def sem(name):
            return ctx.enter_context(nc.semaphore(name))

        x2_d = nc.dram_tensor("x2", [NT * P, D], f32, kind="Internal").ap()
        ys_d = nc.dram_tensor("ys", [ROWS, R], f32, kind="Internal").ap()
        h_d = nc.dram_tensor("h", [QT * 128, R], f32, kind="Internal").ap()
        res_d = nc.dram_tensor("res", [NT * P, D], f32, kind="Internal").ap()
        slot_d = [nc.dram_tensor(f"slot{q}", [NT * P, K], f32, kind="Internal").ap() for q in range(2)]
        wts_d = nc.dram_tensor("wts", [NT * P, 2 * K], f32, kind="Internal").ap()
        zs_d = nc.dram_tensor("zs", [ROWS, D], f32, kind="Internal").ap()

        W = sb("W", [128, NN * 2 * R])
        CST = sb("CST", [128, NC])
        HW = sb("HW", [128, NT * D])
        H = HW[0:P].rearrange("p (t d) -> p t d", d=D)
        HR = HW[:, 0:QT * D].rearrange("p (t d) -> p t d", d=D)
        X2W = sb("X2W", [128, NT * D])
        X2 = X2W[0:P].rearrange("p (t d) -> p t d", d=D)
        XBT = X2W[:, 0:2048].rearrange("p (g c) -> p g c", g=4)
        M = sb("M", [P, NT, 2 * NN], bf16)
        MPRE = sb("MPRE", [P, NT, 2 * NN], bf16)
        XBW = sb("XBW", [128, 8 * D])
        XB = XBW[:].rearrange("p (g a d) -> p g a d", g=4, a=2)
        HOT_HI = XBW[0:P, 0:8 * HI].rearrange("p (j k n) -> p j k n", j=2, k=K)
        TOPA = sb("TOPA", [P, NT, 2, K])
        IDXF = sb("IDXF", [P, NT, 2 * K])
        ZS = sb("ZS", [P, NT, 2])
        WTS = sb("WTS", [P, NT, 2, K])
        WSUM = sb("WSUM", [P, NT, 2])
        SLOT = sb("SLOT", [P, 2, NT, K])
        SLOTR = sb("SLOTR", [128, 2, QT, K])
        WTSR = sb("WTSR", [128, QT, 2, K])
        LOHI = sb("LOHI", [P, 2, 2, K])
        IDST = sb("IDST", [128, 2, K], i32)
        IDG = sb("IDG", [128, 4, 2], i32)
        TAB = sb("TAB", [128, 2, HI], i32)
        HSTG = sb("HSTG", [128, 2, R])
        G = sb("G", [128, 2, K, D])
        YB = [t[0:BS].rearrange("p (b d) -> p b d", d=D) for t in (G[:].rearrange("p j k d -> p (j k d)"), X2W[:, 2048:2048 + 8 * D])]
        JUNK = sb("JUNK", [P, 2, K, NN], bf16)
        HOT_LO = [t[0:P, 0:2 * K * NN].rearrange("p (j k n) -> p j k n", j=2, k=K) for t in (G[:].rearrange("p j k d -> p (j k d)"), X2W)]
        SQ = X2W[0:P, 2 * K * NN:4 * K * NN].rearrange("p (j k n) -> p j k n", j=2, k=K)
        NB = sb("NB", [128, 2], bf16)
        NBF = sb("NBF", [128, 2])
        NBR = sb("NBR", [128, 2, 128], bf16)
        END = sb("END", [128, 2])
        GE = sb("GE", [128, 2, NBLK], bf16)
        ETAB = sb("ETAB", [1, 2, NBLK], i32)
        UB = sb("UB", [128, 128], bf16)
        UIB = sb("UIB", [128, 128], bf16)
        ONES = sb("ONES", [128, 128], bf16)
        THR = sb("THR", [128, MAXB])

        used = [NN * R]

        def front(parts, shape, dt=f32):
            n = 1
            for s in shape:
                n *= s
            words = (n + 1) // 2 if dt == bf16 else n
            a = W[0:parts, used[0]:used[0] + words]
            used[0] += words + words % 2
            assert used[0] <= NN * 2 * R
            if dt != f32:
                a = a.bitcast(dt)
            names = "abcde"[:len(shape)]
            if len(shape) > 1:
                a = a.rearrange(f"p ({' '.join(names)}) -> p {' '.join(names)}", **dict(zip(names[1:], shape[1:])))
            return a

        XT = front(128, [2, KC, P])
        WT = front(128, [KC, D])
        WQKV = front(HC, [2, 3 * D])
        WPROJ = front(HC, [2, D])
        WMID = front(HC, [2, 2 * DS])
        BMID = front(128, [2])
        EMB = front(128, [2 * DS])
        ESQ = front(128, [2 * DS])
        ENS = front(128, [6, 2])
        EBD = front(128, [2 * NN])
        BIASE = front(P, [2, D])
        BPROJ = front(P, [D])
        LNC = front(P, [4])
        Y = front(P, [2, D])
        X2P = front(P, [2, D])
        YT = front(HC, [2, 2, P])
        QK = front(HC, [2, 4, P])
        Q = front(HC, [2, 2, 2, P])
        EX = front(HC, [4, P])
        RX = front(HC, [4, P])
        V32 = front(P, [2, NH, 2 * DH])
        KS = front(HC, [2, IMGS])
        QKS = front(HC, [2, P])
        SM = front(P, [3, 2, 2, P])
        RD = front(HC, [2, P])
        OT = front(HC, [2, 2, P])
        X2T = front(HC, [2, 2, P])
        MID = front(128, [2, P])
        L = front(P, [2, 2 * NN])
        EJ = front(P, [2, NN])
        ST = front(P, [2, 6])
        MV = front(P, [4, 2])
        RS = front(P, [4, 6])
        TOPP = front(P, [2, 2, 8])
        IDXP = front(P, [2, 2, 8], u32)
        IDXS = front(P, [2, 2 * K])
        NM = front(P, [2, 2])
        MP = front(P, [2, NN], bf16)

        ID = CST[:, CI:CI + 128]
        IMASK = CST[0:P, CM:CM + P]
        IOTA = CST[0:P, CO:CO + NN]

        PB = [ps(f"PB{i}") for i in range(8)]
        PE_PROJ, PE_E = PB[0][0:P, 0:D], PB[1][0:P, 0:D]
        PE_YT = PB[3][0:HC, 0:2 * P].rearrange("p (c t) -> p c t", c=2)
        PE_X2T = PB[3][0:HC, 2 * P:4 * P].rearrange("p (c t) -> p c t", c=2)
        PE_QK = PB[2][0:HC, 0:4 * P].rearrange("p (c t) -> p c t", c=4)
        PE_S = [PB[3 + r][0:P, 0:4 * P].rearrange("p (c e t) -> p c e t", c=2, e=2) for r in range(3)]
        PE_V = PB[6][0:P, 0:D]
        PE_O = PB[6][0:HC, 0:2 * P].rearrange("p (c t) -> p c t", c=2)
        PE_DEN = PB[0][0:HC, D:D + 2 * P].rearrange("p (c t) -> p c t", c=2)
        PE_L, PE_MID = PB[7][0:P, 0:2 * NN], PB[7][:, 2 * NN:2 * NN + P]

        names = """loaded consts_in misc_set wt_in eb_sq eb_sum eb_sqrt eb_root_safe eb_inverted eb_quotient eb_newton eb_norm_steps eb_norm eb_T eb_ready
            x_in0 x_in1 emb_done emb_evac st1 stats1 root1_steps rstd1 y_ready yT_done yT_evac qk_done act_qk qk_ready
            v_done v_ready s_done s_masked o_done o_rec oT_ready den_done qmask_ready ks_ready qks_ready pick0 pick1 hb_ready proj_done h2_ready st2 stats2
            root2_steps rstd2 x2_ready x2_kept x2T_done x2T_evac mid_done mid_evac log_done log_evac max_done idx_done
            topk_done idx_kept negmax z_done m_ready mpre_ready
            pads_out f_in f_in_upper r_in x2_stored res_stored res_in slot_stored slot_in wts_stored wts_in cnt_done nb_cmp nb_ready nbr_ready base_done end_ready ge_ready etab_done etab_ready
            shifted exped z_inverted probs_ready wsum_ready wsum_inverted weights_ready
            rank_done slot_ready hi_scaled hi_raised hi_ready lohi_ready lo_diff lo_sq hot_lo hot_hi hot_used tab_ready
            gidx_ready gath0 gath1 comb1 comb2 comb3 hstg_ready h_stored0 h_stored1
            g2idx_ready g2a0 g2a1 comb21 comb22 comb23 out_ready out_stored""".split()
        S = {n: sem(n) for n in names}

        class Stage:
            def __init__(self, n):
                self.idx_ready = sem(f"{n}_idx_ready")
                self.rows_in = [sem(f"{n}_rows_in{i}") for i in range(4)]
                self.rows_T, self.rows_T_evac = sem(f"{n}_rows_T"), sem(f"{n}_rows_T_evac")
                self.mm_done, self.mm_evac = sem(f"{n}_mm_done"), sem(f"{n}_mm_evac")
                self.stored = [sem(f"{n}_stored{i}") for i in range(2)]

        FEAT, REST = Stage("feat"), Stage("rest")
        block = ctx.enter_context(nc.Block())

        def need(eng, s, val):
            if not isinstance(val, int) or val > 0:
                eng.wait_ge(S[s] if isinstance(s, str) else s, val)

        def apart(eng):
            eng.wait_ge(S["consts_in"], 16)

        def tile_loop(eng, body, first, last, head, tail):
            assert (last + 1 - tail - first - head) % 2 == 0 and (first + head) % 2 == 0
            for i in range(first, first + head):
                body(i, i % 2)
            with eng.Fori(0, (last + 1 - tail - first - head) // 2) as u:
                body(u * 2 + (first + head), 0)
                body(u * 2 + (first + head + 1), 1)
            for i in range(last + 1 - tail, last + 1):
                body(i, i % 2)

        def front_loop(eng, body):
            tile_loop(eng, body, 0, NT + 4, 6, 6)

        def on(i, s):
            return not isinstance(i, int) or 0 <= i - s < NT

        def pair_sem(i, j):
            return 8 * (i - j) + 16

        @block.sync
        def _(sp):
            for dst, src in ((WT, wt_d), (BIASE, bias_d)):
                sp.dma_start(dst, src).then_inc(S["wt_in"], 16)
            sp.dma_start(XT[:, 0], xt_d[0]).then_inc(S["x_in0"], 16)
            sp.dma_start(CST[:], const_d).then_inc(S["consts_in"], 16)
            for dst, src in ((WQKV, wqkv_d), (EMB, emb_d)):
                sp.dma_start(dst, src).then_inc(S["loaded"], 16)
            sp.dma_start(XT[:, 1], xt_d[1]).then_inc(S["x_in1"], 16)
            for dst, src in ((WPROJ, wproj_d), (BPROJ, bproj_d), (WMID, wmid_d), (BMID[:, 0:1], bmid_d)):
                sp.dma_start(dst, src).then_inc(S["loaded"], 16)

            def load_x(i, j):
                need(sp, "emb_done", i - 1)
                sp.dma_start(XT[:, j], xt_d[ds(i, 1)].rearrange("a p c t -> (a p) c t")).then_inc(S[f"x_in{j}"], 16)
                if not isinstance(i, int):
                    part = i - 2
                    sp.dma_start(W[0:HC, ds(part * FCOLS, FCOLS)], f_d[:, ds(part * FCOLS, FCOLS)]).then_inc(S["f_in"], 16)

            tile_loop(sp, load_x, 2, NT - 1, 0, 1)

            sp.wait_ge(S["x2_kept"], NT)
            sp.dma_start(x2_d.rearrange("(t p) d -> p t d", p=P), X2).then_inc(S["x2_stored"], 16)
            sp.dma_start(res_d.rearrange("(t p) d -> p t d", p=P), H).then_inc(S["res_stored"], 16)
            sp.wait_ge(S["m_ready"], 2 * NT)
            sp.wait_ge(S["z_done"], NT)
            sp.wait_ge(S["x2_kept"], NT)
            sp.wait_ge(S["idx_kept"], NT)
            sp.wait_ge(S["negmax"], NT)
            for q in (2, 3):
                sp.dma_start(W[0:HC, q * 8192:(q + 1) * 8192], f_d[:, q * 8192:(q + 1) * 8192]).then_inc(S["f_in_upper"], 16)

            def experts(st, dst, n):
                def step(i, j):
                    need(sp, st.mm_evac, 2 * i + 2)
                    sp.dma_start(dst[ds(i * 8 * BS, 8 * BS)].rearrange("(b p) d -> p b d", p=BS),
                                 YB[j][:, :, 0:n]).then_inc(st.stored[j], 16)
                tile_loop(sp, step, 0, ITS - 1, 2, 3)

            def to_128(t):
                return t[0:QT * 128].rearrange("(t p) d -> p t d", p=128)

            def move_slots(q):
                sp.wait_ge(S["slot_ready"], NT * (q + 1))
                sp.dma_start(slot_d[q].rearrange("(t p) k -> p t k", p=P), SLOT[:, q]).then_inc(S["slot_stored"], 16)
                sp.wait_ge(S["slot_stored"], 16 * (q + 1))
                sp.dma_start(SLOTR[:, q], to_128(slot_d[q])).then_inc(S["slot_in"], 16)

            sp.wait_ge(S["res_stored"], 16)
            sp.dma_start(HR, to_128(res_d)).then_inc(S["res_in"], 16)
            move_slots(0)
            sp.wait_ge(S["weights_ready"], 1)
            sp.dma_start(wts_d.rearrange("(t p) k -> p t k", p=P), WTS[:].rearrange("p t q k -> p t (q k)")).then_inc(S["wts_stored"], 16)
            sp.wait_ge(S["wts_stored"], 16)
            sp.dma_start(WTSR[:].rearrange("p t q k -> p t (q k)"), to_128(wts_d)).then_inc(S["wts_in"], 16)
            experts(FEAT, ys_d, R)
            sp.wait_ge(FEAT.mm_done, 2 * ITS)
            def store_h(i, j):
                need(sp, "hstg_ready", i + 1)
                sp.dma_start(h_d[ds(i * 128, 128)], HSTG[:, j]).then_inc(S[f"h_stored{j}"], 16)
                if not isinstance(i, int) or i >= 1:
                    part = i - 1
                    sp.dma_start(W[:, ds(part * RCOLS, RCOLS)], r_d[:, ds(part * RCOLS, RCOLS)]).then_inc(S["r_in"], 16)
            tile_loop(sp, store_h, 0, QT - 1, 2, 1)
            move_slots(1)
            experts(REST, zs_d, D)

            def store(i, j):
                need(sp, "out_ready", i + 1)
                sp.dma_start(out_d[ds(i * 128, 128)], HR[:, ds(i, 1)].rearrange("p a d -> p (a d)")).then_inc(S["out_stored"], 16)
            tile_loop(sp, store, 0, QT - 1, 2, 1)
            sp.wait_ge(S["out_stored"], 16 * QT)

        @block.tensor
        def _(pe):
            mm, tr = nc.tensor.matmul, nc.tensor.transpose
            pe.wait_ge(S["wt_in"], 32)

            def step(i, j):
                a, b, c, d, e, ja, jb, jc, jd, je = i - 1, i - 2, i - 3, i - 4, i - 5, 1 - j, j, 1 - j, j, 1 - j
                if on(i, 1):
                    need(pe, "y_ready", a + 1)
                    need(pe, "x2T_evac", i - 4)
                    need(pe, "s_masked", 3 * (i - 3) + 1)
                    for cc in range(2):
                        last = tr(PE_YT[:, cc], Y[:, ja, cc * HC:(cc + 1) * HC], ID[0:P, 0:P])
                    last.then_inc(S["yT_done"], 1)
                if on(i, 2):
                    need(pe, "qks_ready", b + 1)
                    need(pe, "o_rec", b)
                    need(pe, "h2_ready", i - 3)
                    for cc in range(2):
                        last = mm(PE_DEN[:, cc], CST[0:HC, CG:CG + HC], QKS[:, cc], start=True, stop=True)
                    last.then_inc(S["den_done"], 1)
                if on(i, 3):
                    need(pe, "oT_ready", c + 1)
                    need(pe, "h2_ready", c)
                    for cc in range(2):
                        last = mm(PE_PROJ, OT[:, jc, cc], WPROJ[:, cc], start=(cc == 0), stop=(cc == 1))
                    last.then_inc(S["proj_done"], 1)
                if on(i, 1):
                    need(pe, "yT_evac", a + 1)
                    need(pe, "act_qk", a)
                    for m in range(4):
                        for cc in range(2):
                            last = mm(PE_QK[:, m], WQKV[:, cc, m * HC:(m + 1) * HC], YT[:, ja, cc], start=(cc == 0), stop=(cc == 1))
                    last.then_inc(S["qk_done"], 1)
                    need(pe, "oT_ready", i - 2)
                    for cc in range(2):
                        last = mm(PE_V, YT[:, ja, cc], WQKV[:, cc, 2 * D:3 * D], start=(cc == 0), stop=(cc == 1))
                    last.then_inc(S["v_done"], 1)
                if on(i, 4):
                    need(pe, "x2_ready", d + 1)
                    if not on(i, 1):
                        need(pe, "s_masked", min(3 * (i - 3) + 1, 3 * NT))
                        need(pe, "x2T_evac", d)
                    for cc in range(2):
                        last = tr(PE_X2T[:, cc], X2P[:, jd, cc * HC:(cc + 1) * HC], ID[0:P, 0:P])
                    last.then_inc(S["x2T_done"], 1)
                if on(i, 0):
                    need(pe, S[f"x_in{j}"], pair_sem(i, j))
                    need(pe, "emb_evac", i)
                    for k in range(KC):
                        last = mm(PE_E, XT[:, j, k], WT[:, k], start=(k == 0), stop=(k == KC - 1))
                    last.then_inc(S["emb_done"], 1)
                if on(i, 4):
                    need(pe, "x2T_evac", d + 1)
                    need(pe, "log_evac", d)
                    for cc in range(2):
                        last = mm(PE_MID, WMID[:, cc], X2T[:, jd, cc], start=(cc == 0), stop=(cc == 1))
                    last.then_inc(S["mid_done"], 1)
                if on(i, 2):
                    need(pe, "qmask_ready", b + 1)
                    for r in range(3):
                        need(pe, "s_masked", 3 * (b - 1) + r + 1)
                        if r == 0 and on(i, 4):
                            need(pe, "x2T_evac", d + 1)
                        for cc in range(2):
                            last = mm(PE_S[r][:, cc], QK[32 * r:32 * r + 32, jb, 2 + cc], Q[32 * r:32 * r + 32, jb, cc], start=True, stop=True)
                        last.then_inc(S["s_done"], 1)
                if on(i, 4):
                    need(pe, "mid_evac", d + 1)
                    if isinstance(d, int) and d == 0:
                        pe.wait_ge(S["eb_ready"], 1)
                    mm(PE_L, MID[:, jd], EBD, start=True, stop=True).then_inc(S["log_done"], 1)
                if on(i, 2):
                    need(pe, "v_ready", a + 1 if on(i, 1) else b + 1)
                    if not on(i, 1):
                        need(pe, "oT_ready", b)
                    for r in range(3):
                        need(pe, "s_masked", 3 * b + r + 1)
                        for cc in range(2):
                            for odd in range(2):
                                last = mm(PE_O[32 * r:32 * r + 32, cc], V32[:, jb, 6 * cc + 2 * r + odd], SM[:, r, cc, odd],
                                          start=(odd == 0), stop=(odd == 1))
                    last.then_inc(S["o_done"], 1)
                if isinstance(i, int) and i == 0:
                    pe.wait_ge(S["consts_in"], 16)
                    pe.wait_ge(S["loaded"], 6 * 16)
                if isinstance(i, int) and i == 1:
                    pe.wait_ge(S["eb_norm"], 1)
                    tr(PB[7][:, 0:128], ESQ, ID).then_inc(S["eb_T"], 1)

            front_loop(pe, step)

            pe.wait_ge(S["mpre_ready"], NT - 1)
            pe.wait_ge(S["m_ready"], 2 * NT)
            pe.wait_ge(S["misc_set"], 1)
            for q in range(2):
                mm(PB[0][:, q:q + 1], MPRE[:, NT - 1, q * NN:(q + 1) * NN], ONES[0:P, 0:1], start=True, stop=False)
                last = mm(PB[0][:, q:q + 1], M[:, NT - 1, q * NN:(q + 1) * NN], ONES[0:P, 0:1], start=False, stop=True)
            last.then_inc(S["cnt_done"], 1)
            pe.wait_ge(S["nbr_ready"], 1)
            mm(PB[0][:, 2:4], UIB[:], NB[:], start=True, stop=True).then_inc(S["base_done"], 1)

            def rank(q, i, j):
                need(pe, "slot_ready", i - 1 + q * NT)
                o = PB[2 + j][0:P, 0:NN]
                mm(o, NBR[:, q, 0:P], UB[:], start=True, stop=False)
                mm(o, UB[0:P, 0:P], M[:, ds(i, 1), q * NN:(q + 1) * NN].rearrange("p a n -> p (a n)"), start=False, stop=False)
                mm(o, ONES[0:P, 0:P], MPRE[:, ds(i, 1), q * NN:(q + 1) * NN].rearrange("p a n -> p (a n)"),
                   start=False, stop=True).then_inc(S["rank_done"], 1)

            def table(q, i, j):
                need(pe, "hot_lo", i + 1 + q * NT)
                need(pe, "hot_hi", i + 1 + q * NT)
                for k in range(K):
                    last = mm(PB[1][:, 0:HI], HOT_LO[q][:, j, k], HOT_HI[:, j, k], start=isinstance(i, int) and i + k == 0,
                              stop=isinstance(i, int) and i == NT - 1 and k == K - 1)
                last.then_inc(S["hot_used"], 1)

            def tables(q):
                rank(q, 0, 0)
                rank(q, 1, 1)
                if q == 0:
                    pe.wait_ge(S["ge_ready"], 1)
                    for p in range(2):
                        last = mm(PB[6 + p][0:1, 0:NBLK], UB[:, NN - 1:NN], GE[:, p], start=True, stop=True)
                    last.then_inc(S["etab_done"], 1)

                def step(i, j):
                    if not isinstance(i, int) or i + 2 < NT:
                        rank(q, i + 2, j)
                    if not isinstance(i, int) or i >= 1:
                        table(q, i - 1, 1 - j)
                tile_loop(pe, step, 0, NT - 1, 2, 3)
                table(q, NT - 1, (NT - 1) % 2)
            tables(0)

            def experts(st, q, na, m, n, wcol):
                def turn(i, j, h):
                    need(pe, st.rows_in[2 * j + h], 16 * (i - j) + 32)
                    need(pe, st.rows_T_evac, 2 * i + h - 3)
                    for a in range(2):
                        for cc in range(na):
                            t = a * na + cc
                            last = tr(PB[2 * j + h][0:m, t * 128:(t + 1) * 128], XB[:, 2 * j + h, a, cc * m:(cc + 1) * m], ID)
                    last.then_inc(st.rows_T, 1)

                def product(i, j, h):
                    _, e = nc.values_load_multi_w_load_instructions(ETAB[0:1, q, ds(i * 8 + 4 * h, 4)], engines=[mybir.EngineType.PE],
                                                                    min_val=0, max_val=(NN - 1) * wcol,
                                                                    skip_runtime_bounds_check_because="ETAB is clamped to the last neuron")
                    need(pe, st.rows_T_evac, 2 * i + h + 1)
                    need(pe, st.mm_evac, 2 * i + h - 1)
                    for b in range(4):
                        o = PB[4 + 2 * h + b // 2][0:BS, (b % 2) * n:(b % 2) * n + n]
                        for cc in range(na):
                            col = ((b // 2) * na + cc) * 128 + (b % 2) * BS
                            last = mm(o, XBT[0:m, 2 * j + h, col:col + BS], W[0:m, ds(e[b] + cc * n, n)], start=(cc == 0), stop=(cc == na - 1))
                    last.then_inc(st.mm_done, 1)

                turn(0, 0, 0)

                def step(i, j):
                    turn(i, j, 1)
                    product(i, j, 0)
                    if not isinstance(i, int) or i + 1 < ITS:
                        turn(i + 1, 1 - j, 0)
                    product(i, j, 1)
                tile_loop(pe, step, 0, ITS - 1, 2, 3)

            pe.wait_ge(S["etab_ready"], 1)
            pe.wait_ge(S["f_in"], 16 * PARTS)
            pe.wait_ge(S["f_in_upper"], 32)
            experts(FEAT, 0, 2, HC, R, 2 * R)
            tables(1)
            pe.wait_ge(S["r_in"], 16 * PARTS)
            experts(REST, 1, 1, 128, D, D)

        @block.scalar
        def _(act):
            A = nc.scalar.activation
            act.wait_ge(S["consts_in"], 16)

            def softmax(e, je):
                need(act, "negmax", e + 1)
                need(act, "z_done", e)
                for q in range(2):
                    last = A(EJ[:, q], L[:, je, q * NN:(q + 1) * NN], ACT.Exp, bias=NM[:, je, q:q + 1],
                             accum_out=ZS[:, ds(e, 1), q:q + 1].rearrange("p a q -> p (a q)"))
                last.then_inc(S["z_done"], 1)

            def step(i, j):
                a, b, c, d, e, ja, jb, jc, jd, je = i - 1, i - 2, i - 3, i - 4, i - 5, 1 - j, j, 1 - j, j, 1 - j
                if on(i, 1):
                    need(act, "yT_done", a + 1)
                    need(act, "v_done", a - 1)
                    nc.scalar.copy(YT[:, ja], PE_YT).then_inc(S["yT_evac"], 1)
                if on(i, 5) and on(i, 1):
                    softmax(e, je)
                if on(i, 1):
                    need(act, "qk_done", a + 1)
                    need(act, "qk_ready", a)
                    A(EX, PE_QK, ACT.Exp)
                    A(RX, PE_QK, ACT.Relu).then_inc(S["act_qk"], 1)
                    need(act, "v_done", a + 1)
                    need(act, "o_done", a - 1)
                    if isinstance(a, int) and a == 0:
                        act.wait_ge(S["misc_set"], 1)
                    v32 = V32[:, ja].rearrange("p (h e) d -> p h e d", e=2)
                    v = PE_V.rearrange("p (h e d) -> p h e d", e=2, d=DH)
                    nc.scalar.copy(v32[:, :, 0, 0:DH], v[:, :, 0])
                    nc.scalar.copy(v32[:, :, 1, DH:2 * DH], v[:, :, 1]).then_inc(S["v_ready"], 1)
                if on(i, 4):
                    need(act, "x2T_done", d + 1)
                    need(act, "mid_done", d - 1)
                    nc.scalar.copy(X2T[:, jd], PE_X2T).then_inc(S["x2T_evac"], 1)
                if on(i, 1):
                    need(act, "qk_ready", a + 1)
                    need(act, "s_done", 3 * (a - 1))
                    for odd in range(2):
                        last = A(Q[:, ja, :, odd], QK[:, ja, 0:2], ACT.Copy, scale=CST[0:HC, CE + odd:CE + odd + 1])
                    last.then_inc(S["qmask_ready"], 1)
                if on(i, 4):
                    need(act, "mid_done", d + 1)
                    need(act, "log_done", d - 1)
                    A(MID[:, jd], PE_MID, ACT.Identity, bias=BMID[:, 0:1]).then_inc(S["mid_evac"], 1)
                    need(act, "log_done", d + 1)
                    need(act, "idx_done", d - 1)
                    nc.scalar.copy(L[:, jd], PE_L).then_inc(S["log_evac"], 1)
                if on(i, 5) and not on(i, 1):
                    softmax(e, je)
                if isinstance(i, int) and i == 0:
                    act.wait_ge(S["loaded"], 6 * 16)
                    act.wait_ge(S["eb_sum"], 1)
                    A(ENS[:, 1], ENS[:, 0], ACT.Sqrt).then_inc(S["eb_sqrt"], 1)

            front_loop(act, step)

            act.wait_ge(S["etab_done"], 1)
            for q in range(2):
                last = A(ETAB[:, q], PB[6 + q][0:1, 0:NBLK], ACT.Copy, scale=float((2 * R, D)[q]))
            last.then_inc(S["etab_ready"], 1)

            def tables(q):
                def step(i, j):
                    need(act, "lohi_ready", i + 1 + q * NT)
                    need(act, "hot_lo", i + q * NT)
                    if q == 0:
                        need(act, "lo_diff", i + 1)
                        last = A(SQ[:, j], SQ[:, j], ACT.Square)
                    else:
                        for k in range(K):
                            last = A(SQ[:, j, k], IOTA, ACT.Square, bias=LOHI[:, j, 1, k:k + 1])
                    last.then_inc(S["lo_sq"], 1)
                    need(act, "lo_sq", i + 1 + q * NT)
                    need(act, "hot_used", i - 1 + q * NT)
                    A(HOT_LO[q][:, j], SQ[:, j], ACT.Relu, scale=CST[0:P, ds(CQ + i, 1)], bias=CST[0:P, ds(CR + i, 1)]).then_inc(S["hot_lo"], 1)
                tile_loop(act, step, 0, NT - 1, 2, 3)
            tables(0)

            def experts(st, q, m, w):
                def stage(i, j, h):
                    nc.scalar.copy(IDG[:, 2 * j + h], TAB[:, q, ds(i * 4 + 2 * h, 2)]).then_inc(st.idx_ready, 1)

                act.wait_ge(S["tab_ready"], q + 1)
                for g in range(4):
                    stage(g // 2, g // 2, g % 2)
                if q == 0:
                    act.wait_ge(S["shifted"], 1)
                    A(WTS[:], WTS[:], ACT.Exp).then_inc(S["exped"], 1)

                def step(i, j):
                    for h in range(2):
                        need(act, st.rows_T, 2 * i + h + 1)
                        if not isinstance(i, int) or i + 2 < ITS:
                            stage(i + 2, j, h)
                        need(act, st.mm_done, 2 * i + h - 3)
                        nc.scalar.copy(XBT[0:m, 2 * j + h, 0:w], PB[2 * j + h][0:m, 0:w]).then_inc(st.rows_T_evac, 1)
                tile_loop(act, step, 0, ITS - 1, 2, 3)
            experts(FEAT, 0, HC, 512)
            tables(1)
            experts(REST, 1, 128, 256)

        @block.vector
        def _(dve):
            V = nc.vector
            V.memset(ONES[:], 1.0)
            V.memset(LNC[:, 0:1], -0.5)
            V.memset(LNC[:, 1:2], 1e-5)
            V.memset(LNC[:, 2:3], 1.5)
            V.memset(V32, 0.0)
            V.memset(MPRE[:, 0], 0.0)
            V.memset(EBD, 0.0).then_inc(S["misc_set"], 1)
            dve.wait_ge(S["wt_in"], 32)
            V.tensor_tensor(BIASE[:, 0], BIASE[:, 0], BIASE[:, 1], ALU.add).then_inc(S["misc_set"], 1)
            dve.wait_ge(S["misc_set"], 2)
            dve.wait_ge(S["consts_in"], 16)

            def misc():
                V.tensor_copy(UB[:], CST[:, CU:CU + 128])
                V.tensor_copy(UIB[:], CST[:, CN:CN + 128])

            def embeddings():
                dve.wait_ge(S["loaded"], 6 * 16)
                V.tensor_tensor(ESQ, EMB, EMB, ALU.mult).then_inc(S["eb_sq"], 1)
                dve.wait_ge(S["eb_sq"], 1)
                V.tensor_reduce(ENS[:, 0], ESQ.rearrange("p (q d) -> p q d", q=2), axis=AX.X, op=ALU.add).then_inc(S["eb_sum"], 1)
                dve.wait_ge(S["eb_sqrt"], 1)
                V.tensor_scalar(ENS[:, 2], ENS[:, 1], 1e-30, None, ALU.max).then_inc(S["eb_root_safe"], 1)
                dve.wait_ge(S["eb_root_safe"], 1)
                V.reciprocal(ENS[:, 3], ENS[:, 2]).then_inc(S["eb_inverted"], 1)
                dve.wait_ge(S["eb_inverted"], 1)
                V.tensor_tensor(ENS[:, 3], ENS[:, 3], ENS[:, 0], ALU.mult).then_inc(S["eb_quotient"], 1)
                dve.wait_ge(S["eb_quotient"], 1)
                V.tensor_tensor(ENS[:, 3], ENS[:, 3], ENS[:, 1], ALU.add).then_inc(S["eb_newton"], 1)
                dve.wait_ge(S["eb_newton"], 1)
                V.tensor_scalar(ENS[:, 4], ENS[:, 3], 0.5, 1e-8, ALU.mult, ALU.add).then_inc(S["eb_norm_steps"], 1)
                dve.wait_ge(S["eb_norm_steps"], 1)
                V.reciprocal(ENS[:, 5], ENS[:, 4]).then_inc(S["eb_norm_steps"], 1)
                dve.wait_ge(S["eb_norm_steps"], 2)
                V.tensor_tensor(ESQ.rearrange("p (q d) -> p q d", q=2), EMB.rearrange("p (q d) -> p q d", q=2),
                                ENS[:, 5].rearrange("p (q o) -> p q o", o=1).broadcast_to([128, 2, DS]), ALU.mult).then_inc(S["eb_norm"], 1)

            def row(buf, t):
                return buf[:, ds(t, 1)].rearrange("p a d -> p (a d)")

            def pick(e, je, k):
                for q in range(2):
                    m, at = MP[:, q], IDXS[:, je, q * K + k:q * K + k + 1]
                    if k == 0:
                        need(dve, "m_ready", 2 * e)
                        V.tensor_scalar(m, IOTA, at, None, ALU.is_equal).then_inc(S[f"pick{q}"], 1)
                    else:
                        need(dve, f"pick{q}", e * (K - 1) + k)
                        V.scalar_tensor_tensor(row(M, e)[:, q * NN:(q + 1) * NN] if k == K - 1 else m, IOTA, at, m,
                                               ALU.is_equal, ALU.add).then_inc(S[f"pick{q}" if k < K - 1 else "m_ready"], 1)

            def step(i, j):
                a, b, c, d, e, ja, jb, jc, jd, je = i - 1, i - 2, i - 3, i - 4, i - 5, 1 - j, j, 1 - j, j, 1 - j
                if on(i, 3):
                    need(dve, "o_rec", c + 1)
                    need(dve, "o_done", c + 1)
                    need(dve, "proj_done", c - 1)
                    V.tensor_tensor(OT[:, jc], PE_O, RD, ALU.mult).then_inc(S["oT_ready"], 1)
                if on(i, 5):
                    apart(dve)
                    need(dve, "log_evac", e + 1)
                    apart(dve)
                    for q in range(2):
                        last = V.max(TOPP[:, je, q], L[:, je, q * NN:(q + 1) * NN])
                    last.then_inc(S["max_done"], 1)
                if on(i, 5):
                    need(dve, "max_done", e + 1)
                    need(dve, "z_done", e - 1)
                    V.tensor_scalar(NM[:, je], TOPP[:, je, :, 0], -1.0, None, ALU.mult).then_inc(S["negmax"], 1)
                    for q in range(2):
                        last = V.max_index(IDXP[:, je, q], TOPP[:, je, q], L[:, je, q * NN:(q + 1) * NN])
                    last.then_inc(S["idx_done"], 1)
                if on(i, 4):
                    need(dve, "rstd2", d + 1)
                    need(dve, "x2_kept", d - 1)
                    need(dve, "x2T_done", d - 1)
                    V.tensor_scalar(X2P[:, jd], row(H, d), MV[:, 2 + jd, 0:1], RS[:, 2 + jd, 5:6], ALU.subtract, ALU.mult).then_inc(S["x2_ready"], 1)
                if on(i, 5):
                    V.tensor_copy(TOPA[:, ds(e, 1)].rearrange("p a q k -> p (a q) k"), TOPP[:, je, :, 0:K])
                    need(dve, "idx_done", e + 1)
                    need(dve, "idx_kept", e - 1)
                    last = V.tensor_copy(IDXS[:, je].rearrange("p (q k) -> p q k", q=2), IDXP[:, je, :, 0:K])
                    if isinstance(e, int) and e == NT - 1:
                        last.then_inc(S["pads_out"], 1)
                        dve.wait_ge(S["pads_out"], 1)
                        last = V.tensor_scalar(IDXS[:, je], IDXS[:, je], CST[0:P, CV:CV + 1], CST[0:P, CV + 1:CV + 2], ALU.mult, ALU.add)
                    last.then_inc(S["topk_done"], 1)
                if on(i, 3):
                    need(dve, "proj_done", c + 1)
                    need(dve, "hb_ready", c + 1)
                    need(dve, "rstd2", c - 1)
                    V.tensor_tensor(row(H, c), PE_PROJ, row(H, c), ALU.add).then_inc(S["h2_ready"], 1)
                if on(i, 3):
                    apart(dve)
                    need(dve, "h2_ready", c + 1)
                    apart(dve)
                    V.bn_stats(ST[:, 1], row(H, c)).then_inc(S["st2"], 1)
                if on(i, 2):
                    need(dve, "den_done", b + 1)
                    if on(i, 3):
                        need(dve, "proj_done", c + 1)
                    V.reciprocal(RD, PE_DEN).then_inc(S["o_rec"], 1)
                if on(i, 3):
                    apart(dve)
                    need(dve, "st2", c + 1)
                    apart(dve)
                    V.bn_aggr(MV[:, 2 + jc], ST[:, 1]).then_inc(S["stats2"], 1)
                if on(i, 5):
                    need(dve, "topk_done", e + 1)
                    pick(e, je, 0)
                if on(i, 1):
                    need(dve, "act_qk", a + 1)
                    need(dve, "s_done", 3 * (a - 1))
                    V.scalar_tensor_tensor(QK[:, ja], EX, 1.0, RX, ALU.min, ALU.add).then_inc(S["qk_ready"], 1)
                if on(i, 1):
                    need(dve, "qk_ready", a + 1)
                    V.tensor_reduce(KS, QK[:, ja, 2:4].rearrange("p c (m t) -> p c m t", m=IMGS), axis=AX.X, op=ALU.add).then_inc(S["ks_ready"], 1)
                if on(i, 5):
                    pick(e, je, 1)
                if on(i, 0):
                    need(dve, "rstd1", i - 1)
                    need(dve, "emb_done", i + 1)
                    V.tensor_tensor(row(H, i), PE_E, BIASE[:, 0], ALU.add).then_inc(S["emb_evac"], 1)
                if on(i, 1):
                    need(dve, "ks_ready", a + 1)
                    need(dve, "den_done", a)
                    V.tensor_tensor(QKS.rearrange("p c (m t) -> p (c m) t", m=IMGS), QK[:, ja, 0:2].rearrange("p c (m t) -> p (c m) t", m=IMGS),
                                    KS.rearrange("p c (m o) -> p (c m) o", o=1).broadcast_to([HC, 2 * IMGS, NPOS]),
                                    ALU.mult).then_inc(S["qks_ready"], 1)
                if on(i, 0):
                    apart(dve)
                    need(dve, "emb_evac", i + 1)
                    apart(dve)
                    V.bn_stats(ST[:, 0], row(H, i)).then_inc(S["st1"], 1)
                if on(i, 5):
                    pick(e, je, 2)
                if on(i, 0):
                    apart(dve)
                    need(dve, "st1", i + 1)
                    apart(dve)
                    V.bn_aggr(MV[:, j], ST[:, 0]).then_inc(S["stats1"], 1)

                def mask(r):
                    need(dve, "s_done", 3 * b + r + 1)
                    V.tensor_tensor(SM[:, r].rearrange("p c e t -> p (c e) t"), PE_S[r].rearrange("p c e t -> p (c e) t"),
                                    IMASK.rearrange("p (o t) -> p o t", o=1).broadcast_to([P, 4, P]), ALU.mult).then_inc(S["s_masked"], 1)
                if on(i, 2):
                    need(dve, "o_done", b)
                    mask(0)
                    mask(1)
                if on(i, 5):
                    pick(e, je, 3)
                if on(i, 2):
                    mask(2)
                if on(i, 0):
                    need(dve, "rstd1", i + 1)
                    need(dve, "yT_done", i - 1)
                    V.tensor_scalar(Y[:, j], row(H, i), MV[:, j, 0:1], RS[:, j, 5:6], ALU.subtract, ALU.mult).then_inc(S["y_ready"], 1)
                if isinstance(i, int) and i == 0:
                    misc()
                    embeddings()
                if isinstance(i, int) and i == 1:
                    dve.wait_ge(S["eb_T"], 1)
                    V.tensor_copy(EBD[0:DS, 0:NN], PB[7][0:DS, 0:NN])
                    V.tensor_copy(EBD[DS:128, NN:2 * NN], PB[7][DS:128, 0:NN]).then_inc(S["eb_ready"], 1)

            front_loop(dve, step)

            dve.wait_ge(S["cnt_done"], 1)
            for q in range(2):
                V.tensor_scalar(THR[:], CST[:, CT:CT + MAXB], PB[0][:, q:q + 1], 0.0, ALU.is_lt, ALU.add,
                                accum_out=NBF[:, q:q + 1]).then_inc(S["nb_cmp"], 1)
                dve.wait_ge(S["nb_cmp"], q + 1)
            V.tensor_copy(NB[:], NBF[:]).then_inc(S["nb_ready"], 1)
            for q in range(2):
                last = V.tensor_scalar(NBR[:, q], ONES[:], NBF[:, q:q + 1], float(BS), ALU.mult, ALU.mult)
            last.then_inc(S["nbr_ready"], 1)
            dve.wait_ge(S["base_done"], 1)
            V.tensor_copy(END[:], PB[0][:, 2:4]).then_inc(S["end_ready"], 1)
            dve.wait_ge(S["end_ready"], 1)
            for q in range(2):
                last = V.tensor_scalar(GE[:, q], CST[:, CB:CB + NBLK], END[:, q:q + 1], None, ALU.is_ge)
            last.then_inc(S["ge_ready"], 1)
            def slot(q, i, j, k):
                last = V.scalar_tensor_tensor(JUNK[:, j, k], IOTA, IDXF[:, ds(i, 1), q * K + k:q * K + k + 1].rearrange("p a k -> p (a k)"),
                                              PB[2 + j][0:P, 0:NN], ALU.is_equal, ALU.mult,
                                              accum_out=SLOT[:, q, ds(i, 1), k:k + 1].rearrange("p a k -> p (a k)"))
                if k == K - 1:
                    last.then_inc(S["slot_ready"], 1)

            def first_slots(q):
                dve.wait_ge(S["idx_kept"], NT)
                need(dve, "rank_done", q * NT + 1)
                need(dve, "slot_ready", q * NT)
                for k in range(K):
                    slot(q, 0, 0, k)

            def split(q, i, j):
                n = i + 1 + q * NT
                more = not isinstance(i, int) or i + 1 < NT
                at = SLOT[:, q, ds(i, 1)].rearrange("p a k -> p (a k)")
                hi, lo = LOHI[:, j, 0], LOHI[:, j, 1]
                need(dve, "slot_ready", n)
                need(dve, "lo_sq", n - 2)
                V.tensor_scalar(hi, at, 1 / 128, -63.5 / 128, ALU.mult, ALU.add).then_inc(S["hi_scaled"], 1)
                if more:
                    need(dve, "rank_done", n + 1)
                    slot(q, i + 1, 1 - j, 0)
                need(dve, "hi_scaled", n)
                V.tensor_scalar(hi, hi, MAGIC, None, ALU.add).then_inc(S["hi_raised"], 1)
                if more:
                    slot(q, i + 1, 1 - j, 1)
                need(dve, "hi_raised", n)
                V.tensor_scalar(hi, hi, MAGIC, None, ALU.subtract).then_inc(S["hi_ready"], 1)
                if more:
                    slot(q, i + 1, 1 - j, 2)
                need(dve, "hi_ready", n)
                V.scalar_tensor_tensor(lo, hi, 128.0, at, ALU.mult, ALU.subtract).then_inc(S["lohi_ready"], 1)
                if more:
                    slot(q, i + 1, 1 - j, 3)

            def hot_hi(q, i, j):
                need(dve, "hot_used", i - 1 + q * NT)
                V.tensor_tensor(HOT_HI[:, j], CST[0:P, CB:CB + HI].rearrange("p (o n) -> p o n", o=1).broadcast_to([P, K, HI]),
                                LOHI[:, j, 0].rearrange("p (k o) -> p k o", o=1).broadcast_to([P, K, HI]), ALU.is_equal).then_inc(S["hot_hi"], 1)

            def table(q):
                dve.wait_ge(S["hot_used"], NT * (q + 1))
                V.tensor_copy(TAB[:, q], PB[1][:, 0:HI]).then_inc(S["tab_ready"], 1)

            def tables(q, i, j):
                split(q, i, j)
                hot_hi(q, i, j)
            first_slots(0)
            tile_loop(dve, lambda i, j: tables(0, i, j), 0, NT - 1, 2, 3)
            table(0)

            dve.wait_ge(S["z_done"], NT)
            V.tensor_tensor(WTS[:], TOPA[:], TOPA[:, :, :, 0:1].broadcast_to([P, NT, 2, K]), ALU.subtract).then_inc(S["shifted"], 1)
            V.reciprocal(ZS[:], ZS[:]).then_inc(S["z_inverted"], 1)
            dve.wait_ge(S["exped"], 1)
            dve.wait_ge(S["z_inverted"], 1)

            def over_k(t):
                return t[:].rearrange("p t (q o) -> p t q o", o=1).broadcast_to([P, NT, 2, K])
            V.tensor_tensor(WTS[:], WTS[:], over_k(ZS), ALU.mult).then_inc(S["probs_ready"], 1)
            dve.wait_ge(S["probs_ready"], 1)
            V.tensor_reduce(WSUM[:], WTS[:], axis=AX.X, op=ALU.add).then_inc(S["wsum_ready"], 1)
            dve.wait_ge(S["wsum_ready"], 1)
            V.tensor_scalar(WSUM[:], WSUM[:], 1e-8, None, ALU.add).then_inc(S["wsum_ready"], 1)
            dve.wait_ge(S["wsum_ready"], 2)
            V.reciprocal(WSUM[:], WSUM[:]).then_inc(S["wsum_inverted"], 1)
            dve.wait_ge(S["wsum_inverted"], 1)
            V.tensor_tensor(WTS[:], WTS[:], over_k(WSUM), ALU.mult).then_inc(S["weights_ready"], 1)

            def experts(st, n):
                def step(i, j):
                    if not isinstance(i, int) or i >= 2:
                        dve.wait_ge(st.stored[j], 8 * (i - j))
                    for h in range(2):
                        need(dve, st.mm_done, 2 * i + h + 1)
                        for u in range(2):
                            last = V.tensor_copy(YB[j][:, 4 * h + 2 * u:4 * h + 2 * u + 2, 0:n],
                                                 PB[4 + 2 * h + u][0:BS, 0:2 * n].rearrange("p (b n) -> p b n", b=2))
                        last.then_inc(st.mm_evac, 1)
                tile_loop(dve, step, 0, ITS - 1, 2, 3)

            experts(FEAT, R)
            dve.wait_ge(S["weights_ready"], 1)

            def idx1(i, j):
                if not isinstance(i, int) or i >= 2:
                    dve.wait_ge(S[f"gath{j}"], 32 * (i - j))
                V.tensor_copy(IDST[:, j], SLOTR[:, 0, ds(i, 1)].rearrange("p a k -> p (a k)")).then_inc(S["gidx_ready"], 1)

            def weight(i, q, k):
                return WTSR[:, ds(i, 1), q, k:k + 1].rearrange("p a k -> p (a k)")

            def combine1(i, j):
                dve.wait_ge(S[f"gath{j}"], 32 * (i - j) + 64)
                if not isinstance(i, int) or i >= 2:
                    dve.wait_ge(S[f"h_stored{j}"], 8 * (i - j))
                g, h = G[:, j], HSTG[:, j]
                V.tensor_scalar(h, g[:, 0, 0:R], weight(i, 0, 0), None, ALU.mult).then_inc(S["comb1"], 1)
                need(dve, "comb1", i + 1)
                V.scalar_tensor_tensor(h, g[:, 1, 0:R], weight(i, 0, 1), h, ALU.mult, ALU.add).then_inc(S["comb2"], 1)
                need(dve, "comb2", i + 1)
                V.scalar_tensor_tensor(h, g[:, 2, 0:R], weight(i, 0, 2), h, ALU.mult, ALU.add).then_inc(S["comb3"], 1)
                need(dve, "comb3", i + 1)
                V.scalar_tensor_tensor(h, g[:, 3, 0:R], weight(i, 0, 3), h, ALU.mult, ALU.add).then_inc(S["hstg_ready"], 1)

            dve.wait_ge(S["slot_in"], 16)
            dve.wait_ge(S["wts_in"], 16)
            idx1(0, 0)
            idx1(1, 1)
            first_slots(1)
            for i in range(4):
                tables(1, i, i % 2)

            def middle(i, j):
                combine1(i, j)
                if not isinstance(i, int) or i + 2 < QT:
                    idx1(i + 2, j)
                if not isinstance(i, int) or i + 4 < NT:
                    tables(1, i + 4, j)
            tile_loop(dve, middle, 0, QT - 1, 2, 3)
            table(1)

            experts(REST, D)

            def idx2(i, j):
                if not isinstance(i, int) or i >= 2:
                    dve.wait_ge(S[f"g2a{j}"], 32 * (i - j))
                V.tensor_copy(IDST[:, j], SLOTR[:, 1, ds(i, 1)].rearrange("p a k -> p (a k)")).then_inc(S["g2idx_ready"], 1)

            def finish(i, j):
                dve.wait_ge(S[f"g2a{j}"], 32 * (i - j) + 64)
                for k in range(K):
                    last = V.scalar_tensor_tensor(row(HR, i), G[:, j, k], weight(i, 1, k), row(HR, i), ALU.mult, ALU.add)
                    if k < K - 1:
                        last.then_inc(S[f"comb2{k + 1}"], 1)
                        need(dve, f"comb2{k + 1}", i + 1)
                last.then_inc(S["out_ready"], 1)
                if not isinstance(i, int) or i + 2 < QT:
                    idx2(i + 2, j)
            dve.wait_ge(S["slot_in"], 32)
            dve.wait_ge(S["res_in"], 16)
            idx2(0, 0)
            idx2(1, 1)
            tile_loop(dve, finish, 0, QT - 1, 2, 3)

        @block.gpsimd
        def _(pool):
            GP = nc.gpsimd
            pool.wait_ge(S["consts_in"], 16)
            pool.wait_ge(S["misc_set"], 1)

            def rstd(m, r, s, t):
                def c(k):
                    return RS[:, r, k:k + 1]
                GP.tensor_tensor(c(0), MV[:, m, 1:2], LNC[:, 1:2], ALU.add).then_inc(S[s], 1)
                need(pool, s, 6 * t + 1)
                GP.tensor_tensor(c(1), c(0), LNC[:, 0:1], ALU.pow).then_inc(S[s], 1)
                need(pool, s, 6 * t + 2)
                GP.tensor_tensor(c(2), c(1), c(1), ALU.mult).then_inc(S[s], 1)
                need(pool, s, 6 * t + 3)
                GP.tensor_tensor(c(3), c(2), c(0), ALU.mult).then_inc(S[s], 1)
                need(pool, s, 6 * t + 4)
                GP.tensor_tensor(c(4), c(3), LNC[:, 0:1], ALU.mult).then_inc(S[s], 1)
                need(pool, s, 6 * t + 5)
                GP.tensor_tensor(c(3), c(4), LNC[:, 2:3], ALU.add).then_inc(S[s], 1)
                need(pool, s, 6 * t + 6)
                GP.tensor_tensor(c(5), c(3), c(1), ALU.mult).then_inc(S["rstd" + s[4]], 1)

            def step(i, j):
                a, b, c, d, e, ja, jb, jc, jd, je = i - 1, i - 2, i - 3, i - 4, i - 5, 1 - j, j, 1 - j, j, 1 - j
                if on(i, 4):
                    need(pool, "x2_ready", d + 1)
                    GP.tensor_copy(X2[:, ds(d, 1)].rearrange("p a d -> p (a d)"), X2P[:, jd]).then_inc(S["x2_kept"], 1)
                if on(i, 3):
                    need(pool, "stats2", c + 1)
                    need(pool, "x2_ready", c - 1)
                    rstd(2 + jc, 2 + jc, "root2_steps", c)
                if on(i, 5):
                    need(pool, "topk_done", e + 1)
                    GP.tensor_copy(IDXF[:, ds(e, 1)].rearrange("p a k -> p (a k)"), IDXS[:, je]).then_inc(S["idx_kept"], 1)
                if on(i, 2):
                    need(pool, "y_ready", b + 1)
                    h = H[:, ds(b, 1)].rearrange("p a d -> p (a d)")
                    GP.tensor_tensor(h, h, BPROJ, ALU.add).then_inc(S["hb_ready"], 1)
                if on(i, 0):
                    need(pool, "stats1", i + 1)
                    need(pool, "y_ready", i - 1)
                    rstd(j, j, "root1_steps", i)
                if on(i, 5) and not (isinstance(e, int) and e == NT - 1):
                    need(pool, "m_ready", 2 * e + 2)
                    need(pool, "mpre_ready", e)
                    GP.tensor_tensor(MPRE[:, ds(e + 1, 1)].rearrange("p a n -> p (a n)"), MPRE[:, ds(e, 1)].rearrange("p a n -> p (a n)"),
                                     M[:, ds(e, 1)].rearrange("p a n -> p (a n)"), ALU.add).then_inc(S["mpre_ready"], 1)

            front_loop(pool, step)

            def bound(rows, n):
                return rows - 1 + n

            def off(ids, j, k):
                return bass.IndirectOffsetOnAxis(ap=ids[:, j, k:k + 1], axis=0)

            def experts(st, src, n):
                def step(i, j):
                    for h in range(2):
                        need(pool, st.idx_ready, 2 * i + h + 1)
                        for a in range(2):
                            pool.indirect_dma_start(out=XB[:, 2 * j + h, a, 0:n], out_offset=None, in_=src, in_offset=off(IDG, 2 * j + h, a),
                                                    bounds_check=bound(QT * 128, 2 * i + h), oob_is_err=False).then_inc(st.rows_in[2 * j + h], 16)
                tile_loop(pool, step, 0, ITS - 1, 2, 3)

            def lo_diff(i, j):
                need(pool, "lohi_ready", i + 1)
                need(pool, "hot_lo", i - 1)
                GP.tensor_tensor(SQ[:, j], IOTA.rearrange("p (o n) -> p o n", o=1).broadcast_to([P, K, NN]),
                                 LOHI[:, j, 1].rearrange("p (k o) -> p k o", o=1).broadcast_to([P, K, NN]), ALU.add).then_inc(S["lo_diff"], 1)
            pool.wait_ge(S["x2_stored"], 16)
            tile_loop(pool, lo_diff, 0, NT - 1, 2, 3)

            experts(FEAT, x2_d, D)

            pool.wait_ge(FEAT.stored[0], 16 * ((ITS + 1) // 2))
            pool.wait_ge(FEAT.stored[1], 16 * (ITS // 2))

            def gather_y(i, j):
                need(pool, "gidx_ready", i + 1)
                need(pool, "hstg_ready", i - 1)
                for k in range(K):
                    pool.indirect_dma_start(out=G[:, j, k, 0:R], out_offset=None, in_=ys_d, in_offset=off(IDST, j, k),
                                            bounds_check=bound(ROWS, i), oob_is_err=False).then_inc(S[f"gath{j}"], 16)

            tile_loop(pool, gather_y, 0, QT - 1, 2, 1)
            pool.wait_ge(S["h_stored0"], 16 * ((QT + 1) // 2))
            pool.wait_ge(S["h_stored1"], 16 * (QT // 2))
            experts(REST, h_d, R)

            pool.wait_ge(REST.stored[0], 16 * ((ITS + 1) // 2))
            pool.wait_ge(REST.stored[1], 16 * (ITS // 2))

            def gather_z(i, j):
                need(pool, "g2idx_ready", i + 1)
                need(pool, "out_ready", i - 1)
                for k in range(K):
                    pool.indirect_dma_start(out=G[:, j, k], out_offset=None, in_=zs_d, in_offset=off(IDST, j, k),
                                            bounds_check=bound(ROWS, i), oob_is_err=False).then_inc(S[f"g2a{j}"], 16)
            tile_loop(pool, gather_z, 0, QT - 1, 2, 1)


def kernel(x, cls_tok, L0_tok_W, L0_tok_b, L0_tok_pos, L0_attn_w_qkv, L0_attn_w_proj, L0_attn_b_proj, L0_ffn_f_know,
           L0_ffn_r_know, L0_ffn_W_fk, L0_ffn_b_fk, L0_ffn_W_rk, L0_ffn_b_rk, L0_ffn_emb_fk, L0_ffn_emb_rk):
    import numpy as np
    import concourse.bacc as bacc
    from concourse.bass_utils import run_bass_kernel_spmd as run

    a = np.asarray
    nimg = NT * IMGS
    p = a(x).reshape(B, 3, 4, 16, 4, 16).transpose(0, 2, 4, 1, 3, 5).reshape(B, 16, 768)
    xt = np.zeros((nimg, NPOS, 768), np.float32)
    xt[:B, 1:] = p
    xt = xt.reshape(NT, P, KC, 128).transpose(0, 3, 2, 1)

    def halves(w):
        return w.reshape(2, HC, -1).transpose(1, 0, 2)

    bias = np.zeros((IMGS, NPOS, 2, D), np.float32)
    bias[:, 0, 0] = a(cls_tok).reshape(1, D)
    bias[:, 1:, 0] = a(L0_tok_pos).reshape(1, 16, D)
    bias[:, 1:, 1] = a(L0_tok_b)
    arrays = {
        "xt": xt,
        "wt": a(L0_tok_W).T.reshape(KC, 128, D).transpose(1, 0, 2),
        "bias": bias.reshape(P, 2, D),
        "wqkv": halves(a(L0_attn_w_qkv).T),
        "wproj": halves(a(L0_attn_w_proj).T),
        "bproj": np.broadcast_to(a(L0_attn_b_proj), (P, D)),
        "wmid": halves(np.concatenate([a(L0_ffn_W_fk), a(L0_ffn_W_rk)], axis=1)),
        "bmid": np.concatenate([a(L0_ffn_b_fk), a(L0_ffn_b_rk)]).reshape(128, 1),
        "emb": np.concatenate([a(L0_ffn_emb_fk), a(L0_ffn_emb_rk)], axis=1),
        "fknow": a(L0_ffn_f_know).reshape(NN, 2, HC, R).transpose(2, 0, 1, 3).reshape(HC, NN * 2 * R),
        "rknow": a(L0_ffn_r_know).transpose(1, 0, 2).reshape(R, NN * D),
        "const": constants(np),
    }
    arrays = {k: np.ascontiguousarray(v) for k, v in arrays.items()}
    nc = bacc.Bacc("TRN2", target_bir_lowering=False, num_devices=1)
    args = [nc.dram_tensor(k, v.shape, mybir.dt.from_np(v.dtype), kind="ExternalInput").ap() for k, v in arrays.items()]
    out = nc.dram_tensor("out", [B * NPOS, D], mybir.dt.float32, kind="ExternalOutput").ap()
    vit_block(nc, *args, out)
    got = run(nc, [arrays], core_ids=[0]).results[0]["out"]
    return np.asarray(got).reshape(B, NPOS, D)
```
